# Optimizing a Trainium2 kernel written in Bass

```python
import numpy as np
import jax
import jax.numpy as jnp

def _softmax(x, axis=-1):
    return jax.nn.softmax(x, axis=axis)

def _gelu(x):
    return jax.nn.gelu(x, approximate=True)

def _silu(x):
    return jax.nn.silu(x)

def _sigmoid(x):
    return jax.nn.sigmoid(x)

def _layernorm(x, axis=-1, eps=1e-05):
    m = jnp.mean(x, axis=axis, keepdims=True)
    v = jnp.var(x, axis=axis, keepdims=True)
    return (x - m) / jnp.sqrt(v + eps)

def _scatter_add(tgt, idx, src, axis=0):
    return tgt.at[idx].add(src)

def _segment_sum(src, seg, n):
    return jax.ops.segment_sum(src, seg, n)
kernel_name = 'mk_flamingo_gated_d1_seqx_r2_9a6f6f'

def setup_inputs(seed: int=0):
    np.random.seed(seed)
    _w = jnp.asarray

    def _rec_inputs():
        import jax
        import jax.numpy as jnp
        _rk = jax.random.key(seed)
        x = 2.818e-05 + 1 * jax.random.normal(jax.random.fold_in(_rk, 1), (4, 1024, 1024), jnp.float32)
        _lenS = 1024 - jax.random.randint(jax.random.fold_in(_rk, 7), (4,), 0, max(1, 1024 // 4) + 1, jnp.int32)
        _lenS2 = 1024 - jax.random.randint(jax.random.fold_in(_rk, 8), (4,), 0, max(1, 1024 // 4) + 1, jnp.int32)
        _ctx_1024P = jax.random.normal(jax.random.fold_in(_rk, 11), (4, 16, 512), jnp.float32)
        _ctx_1024c = jax.random.dirichlet(jax.random.fold_in(_rk, 511), 0.3 * jnp.ones((16,), jnp.float32), (4, 1024))
        _ctx_1024t = jnp.einsum('bsk,bkd->bsd', _ctx_1024c, _ctx_1024P)
        _ctx_1024t = _ctx_1024t * jax.lax.rsqrt(jnp.mean(jnp.square(_ctx_1024t)) + 1e-12) * 0.953939
        ctx_1024 = 7.22013e-05 + 1.00017 * (_ctx_1024t + 0.3 * jax.random.normal(jax.random.fold_in(_rk, 611), (4, 1024, 512), jnp.float32))
        _g = jax.random.normal(jax.random.fold_in(_rk, 9001), (2, 1), jnp.float32)
        _g = jnp.sign(_g) * jnp.maximum(jnp.abs(_g), 1.0) + (_g == 0) * 1.0
        g_xattn = _g[0]
        g_ffn = _g[1]
        return (x, ctx_1024, g_xattn, g_ffn)
    x, ctx_1024, g_xattn, g_ffn = _rec_inputs()

    def _L0_xattn_setup():
        import jax, jax.numpy as jnp
        import numpy as np
        B_, L_, D_MODEL = (4, 1024, 512)
        D_STATE, D_CONV, EXPAND = (16, 4, 2)
        D_INNER = EXPAND * D_MODEL
        DT_RANK = (D_MODEL + 15) // 16

        def silu(x):
            return x * jax.nn.sigmoid(x)
        key = jax.random.key(seed)
        ks = jax.random.split(key, 10)
        f32 = jnp.float32
        hidden_states = jax.random.normal(ks[0], (B_, L_, D_MODEL), dtype=f32)
        z = jax.random.normal(ks[1], (B_, D_INNER, L_), dtype=f32)
        in_proj_w = jax.random.normal(ks[2], (D_INNER, D_MODEL), dtype=f32) * 0.02
        conv_w = jax.random.normal(ks[3], (D_INNER, 1, D_CONV), dtype=f32) * 0.1
        conv_b = jax.random.normal(ks[4], (D_INNER,), dtype=f32) * 0.02
        x_proj_w = jax.random.normal(ks[5], (DT_RANK + 2 * D_STATE, D_INNER), dtype=f32) * 0.02
        dt_proj_w = jax.random.uniform(ks[6], (D_INNER, DT_RANK), dtype=f32, minval=-DT_RANK ** (-0.5), maxval=DT_RANK ** (-0.5))
        dt = jnp.exp(jax.random.uniform(ks[7], (D_INNER,), dtype=f32, minval=np.log(0.001), maxval=np.log(0.1)))
        dt_proj_b = jnp.log(jnp.expm1(dt))
        A_log = jnp.log(jnp.broadcast_to(jnp.arange(1, D_STATE + 1, dtype=f32), (D_INNER, D_STATE)))
        D = jnp.ones((D_INNER,), f32)
        return {'hidden_states': hidden_states, 'z': z, 'in_proj_w': in_proj_w, 'conv_w': conv_w, 'conv_b': conv_b, 'x_proj_w': x_proj_w, 'dt_proj_w': dt_proj_w, 'dt_proj_b': dt_proj_b, 'A_log': A_log, 'D': D}
    _L0_xattn_all = _L0_xattn_setup()
    _L0_xattn_in = {k: v for k, v in _L0_xattn_all.items() if k in ('in_proj_w', 'conv_w', 'conv_b', 'x_proj_w', 'dt_proj_w', 'dt_proj_b', 'A_log', 'D')}
    del _L0_xattn_all

    def _L0_ffn_setup():
        import jax, jax.numpy as jnp
        import numpy as np
        NUM_EXPERTS = 16
        C = 1.0
        key = jax.random.key(seed)
        k1, k2, k3 = jax.random.split(key, 3)
        b, s, h = (4, 1024, 1024)
        return {'x': jax.random.normal(k1, (b, s, h), dtype=jnp.float32), 'router_w': jax.random.normal(k2, (h, NUM_EXPERTS), dtype=jnp.float32) * 0.02, 'router_b': jnp.zeros((NUM_EXPERTS,), dtype=jnp.float32), 'expert_w': jax.random.normal(k3, (h, h), dtype=jnp.float32) * 0.02, 'expert_b': jnp.zeros((h,), dtype=jnp.float32)}
    _L0_ffn_all = _L0_ffn_setup()
    _L0_ffn_in = {k: v for k, v in _L0_ffn_all.items() if k in ('router_w', 'router_b', 'expert_w', 'expert_b')}
    del _L0_ffn_all
    return {'x': x, 'ctx_1024': ctx_1024, 'g_xattn': g_xattn, 'g_ffn': g_ffn, 'L0_xattn_in_proj_w': _L0_xattn_in['in_proj_w'], 'L0_xattn_conv_w': _L0_xattn_in['conv_w'], 'L0_xattn_conv_b': _L0_xattn_in['conv_b'], 'L0_xattn_x_proj_w': _L0_xattn_in['x_proj_w'], 'L0_xattn_dt_proj_w': _L0_xattn_in['dt_proj_w'], 'L0_xattn_dt_proj_b': _L0_xattn_in['dt_proj_b'], 'L0_xattn_A_log': _L0_xattn_in['A_log'], 'L0_xattn_D': _L0_xattn_in['D'], 'L0_ffn_router_w': _L0_ffn_in['router_w'], 'L0_ffn_router_b': _L0_ffn_in['router_b'], 'L0_ffn_expert_w': _L0_ffn_in['expert_w'], 'L0_ffn_expert_b': _L0_ffn_in['expert_b']}

def reference(x, ctx_1024, g_xattn, g_ffn, L0_xattn_in_proj_w, L0_xattn_conv_w, L0_xattn_conv_b, L0_xattn_x_proj_w, L0_xattn_dt_proj_w, L0_xattn_dt_proj_b, L0_xattn_A_log, L0_xattn_D, L0_ffn_router_w, L0_ffn_router_b, L0_ffn_expert_w, L0_ffn_expert_b):
    import jax
    import jax.numpy as jnp

    def _L0_xattn_ref(hidden_states, z, in_proj_w, conv_w, conv_b, x_proj_w, dt_proj_w, dt_proj_b, A_log, D):
        import jax, jax.numpy as jnp
        import numpy as np
        B_, L_, D_MODEL = (4, 1024, 512)
        D_STATE, D_CONV, EXPAND = (16, 4, 2)
        D_INNER = EXPAND * D_MODEL
        DT_RANK = (D_MODEL + 15) // 16

        def silu(x):
            return x * jax.nn.sigmoid(x)
        Bsz, L, _ = hidden_states.shape
        d_inner, _, d_conv = conv_w.shape
        dt_rank = dt_proj_w.shape[1]
        d_state = A_log.shape[1]
        x = jnp.einsum('bld,ed->bel', hidden_states, in_proj_w)
        xc = jax.lax.conv_general_dilated(x, conv_w, window_strides=(1,), padding=[(d_conv - 1, 0)], feature_group_count=d_inner, dimension_numbers=('NCH', 'OIH', 'NCH'))
        x = silu(xc + conv_b[None, :, None])
        x_dbl = jnp.einsum('bdl,ed->bel', x, x_proj_w)
        dt_low, Bm, Cm = jnp.split(x_dbl, [dt_rank, dt_rank + d_state], axis=1)
        dt = jnp.einsum('brl,dr->bdl', dt_low, dt_proj_w)
        dt = jax.nn.softplus(dt + dt_proj_b[None, :, None])
        A = -jnp.exp(A_log)
        dt_t = jnp.moveaxis(dt, -1, 0)
        B_t = jnp.moveaxis(Bm, -1, 0)
        C_t = jnp.moveaxis(Cm, -1, 0)
        u_t = jnp.moveaxis(x, -1, 0)

        def step(state, inp):
            d, b, c, u = inp
            dA = jnp.exp(d[..., None] * A)
            state = state * dA + (d * u)[..., None] * b[:, None, :]
            y = jnp.einsum('bdn,bn->bd', state, c)
            return (state, y)
        state0 = jnp.zeros((Bsz, d_inner, d_state), x.dtype)
        _, ys = jax.lax.scan(step, state0, (dt_t, B_t, C_t, u_t))
        y = jnp.moveaxis(ys, 0, 2)
        y = y + D[None, :, None] * x
        y = y * silu(z)
        return jnp.swapaxes(y, 1, 2)

    def _L0_ffn_ref(x, router_w, router_b, expert_w, expert_b):
        import jax, jax.numpy as jnp
        import numpy as np
        NUM_EXPERTS = 16
        C = 1.0
        b, s, h = x.shape
        bs = b * s
        k = min(int(bs * C / NUM_EXPERTS), bs)
        xf = x.reshape(bs, h)
        logits = xf @ router_w + router_b
        S = jax.nn.softmax(logits, axis=-1)
        G, idx = jax.lax.top_k(S.T, k)
        tokens = xf[idx]
        out = jnp.einsum('ekh,hd->ekd', tokens, expert_w) + expert_b
        weighted = G[..., None] * out
        y = jnp.zeros((bs, h), dtype=x.dtype).at[idx.reshape(-1)].add(weighted.reshape(-1, h))
        return y.reshape(b, s, h)
    x = x + jnp.tanh(g_xattn[0]) * _L0_xattn_ref(ctx_1024, _layernorm(x, axis=-1), L0_xattn_in_proj_w, L0_xattn_conv_w, L0_xattn_conv_b, L0_xattn_x_proj_w, L0_xattn_dt_proj_w, L0_xattn_dt_proj_b, L0_xattn_A_log, L0_xattn_D)
    x = x + jnp.tanh(g_ffn[0]) * _L0_ffn_ref(_layernorm(x, axis=-1), L0_ffn_router_w, L0_ffn_router_b, L0_ffn_expert_w, L0_ffn_expert_b)
    return x

_drawn_inputs = setup_inputs


def setup_inputs(seed=0):
    import zlib

    import numpy as np

    out = dict(_drawn_inputs(seed))
    spreads = {'L0_xattn_D': (1.0, 0.6), 'L0_ffn_router_b': (0.0, 0.513), 'L0_ffn_expert_b': (0.0, 0.409)}
    factors = {'L0_xattn_conv_b': 7.908,
     'L0_xattn_x_proj_w': 8.0,
     'L0_xattn_dt_proj_w': 8.0,
     'L0_xattn_dt_proj_b': 8.0,
     'L0_xattn_A_log': 8.0}
    for name, (base, spread) in spreads.items():
        noise = np.random.default_rng([zlib.crc32(name.encode()), seed]).standard_normal(out[name].shape)
        drawn = base * np.exp(spread * noise) if base else spread * noise
        out[name] = jnp.asarray(drawn.astype(out[name].dtype))
    for name, factor in factors.items():
        out[name] = (out[name] * factor).astype(out[name].dtype)
    return out
```

```python
from contextlib import ExitStack

import numpy as np
import concourse.bass as bass
from concourse import mybir

ALU = mybir.AluOpType
ACT = mybir.ActivationFunctionType
AX = mybir.AxisListType
F32 = mybir.dt.float32
U32 = mybir.dt.uint32

P = 128
B, L, D = 4, 1024, 1024
DM = 512
KC = DM // P
E = D // P
NS = 16
R = 32
TAPS = 4
HB = 2
T = L // HB
TT = T // P
NC = B * HB
NX = 16
TOPK = B * L // NX
EPS = 1e-5
GN = 2
GQ = NS // GN
G = E * GQ
NST = 3
BITS = 30
HALO = TAPS - 1

IN_SLOT = [2 + 5 * j for j in range(E)]
CONV_SLOT = [s + 2 for s in IN_SLOT]
SILU_SLOT, XP_SLOT, LOW_SLOT = 42, 43, 50
SZ_SLOT = 8
Y_SLOT = [8 * (e + 1) + 1 for e in range(E - 1)] + [1]
YT_SLOT = [12, 25, 29, 36, 44, 52, 60, 3]
RES_SLOT = [24, 26, 30, 37, 45, 53, 61, 4]
LN2_SLOT = 6
XF_SLOT = 10
XFP_SLOT = [11 + f for f in range(2 * TT)]
LG_SLOT = [14 + 2 * t for t in range(TT)]
SM_SLOT = 25


def n(b, o, K, k):
    return b * (HB * K) + (o * K + k)


def wait(eng, sem, value):
    if not (isinstance(value, int) and value <= 0):
        eng.wait_ge(sem, value)


def mamba_moe(nc, x, ctxT, g_xattn, g_ffn, winT, conv_w, conv_b, xpT, dtpT, dt_b, a_log, dvec,
              router_w, router_b, expert_w, expert_b, consts, out):
    with ExitStack() as ctx:
        def sb(name, shape, dt=F32):
            return ctx.enter_context(nc.sbuf_tensor(name, shape, dt))

        def bank(name):
            return ctx.enter_context(nc.psum_tensor(name, [P, 512], F32))

        def sem(name):
            return ctx.enter_context(nc.semaphore(name))

        bc_dram = nc.dram_tensor("bc_scratch", [NC + 1, 2 * NS, T], F32, kind="Internal").ap()
        x2_dram = nc.dram_tensor("x2_scratch", [NC, P, TT, D], F32, kind="Internal").ap()
        xfT_dram = nc.dram_tensor("xfT_scratch", [NC, TT, P, E * P], F32, kind="Internal").ap()

        win = [sb(f"win{i}", [P, KC, P]) for i in range(2)]
        xp = sb("xp", [P, E, 2 * R])
        dtp = sb("dtp", [R, D])
        cw = sb("cw", [P, E, TAPS])
        cb = sb("cb", [P, E])
        dtb = sb("dtb", [P, E])
        al = sb("al", [P, E * NS])
        an = sb("an", [P, E * NS])
        dv = sb("dv", [P, E])
        rw = sb("rw", [P, E, NX])
        rb = sb("rb", [P, TT, NX])
        gg = sb("gg", [P, 2])
        tg = sb("tg", [P, 2])
        con = sb("con", [P, 3 * P + NC])
        ident = con[:, 0:P]
        same_expert = con[:, P:2 * P]
        earlier = con[:, 2 * P:3 * P]
        seg_of = con[:, 3 * P:3 * P + NC]
        zero3 = sb("zero3", [P, HALO])
        mhalf = sb("mhalf", [P, B, E])
        ctx_sb = sb("ctx_sb", [P, KC, T])
        xt = sb("xt", [P, TT, D])
        sz = sb("sz", [P, E, T])
        xin = [sb(f"xin{i}", [P, HALO + T]) for i in range(2)]
        halo = sb("halo", [P, E, HALO])
        u = [sb(f"u{i}", [P, E, T]) for i in range(2)]
        sp3 = sb("sp3", [P, 3, T])
        dt = [sb(f"dt{i}", [P, T]) for i in range(2)]
        dtu = [sb(f"dtu{i}", [P, T]) for i in range(2)]
        y = [sb(f"y{i}", [P, T]) for i in range(2)]
        xpr = sb("xpr", [2 * R, T])
        bbc = sb("bbc", [P, NS, T])
        cbc = sb("cbc", [P, NS, T])
        decay = [sb(f"decay{i}", [P, GN, T]) for i in range(2)]
        states = [sb(f"states{i}", [P, GN, T]) for i in range(NST)]
        carry = sb("carry", [P, E, NS])
        xfT = [sb(f"xfT{i}", [P, E, P]) for i in range(2)]
        stats = [sb(f"stats{i}", [P, TT, 2, 6]) for i in range(2)]
        mv1 = sb("mv1", [P, B, E, 2])
        ve1 = sb("ve1", [P, B, E])
        ln1 = sb("ln1", [P, B, 2, E])
        cur = sb("cur", [P, 2, E])
        mv2 = sb("mv2", [P, TT, 2])
        ve2 = sb("ve2", [P, TT])
        rs2 = sb("rs2", [P, TT])
        nb2 = sb("nb2", [P, TT])
        lg = sb("lg", [P, TT, NX])
        mx = sb("mx", [P, TT])
        sm = sb("sm", [P, TT])
        rc = sb("rc", [P, TT])
        S_tok = sb("S_tok", [P, TT, NC, NX])
        small = sb("small", [P, 16])
        bits = sb("bits", [P, 4], U32)
        coef = sb("coef", [P, TT, NC])

        pA = [bank("pA0"), bank("pA1")]
        pD = bank("pD")
        pY = [bank("pY0"), bank("pY1")]
        pT = bank("pT")
        pF = bank("pF")
        pL = bank("pL")

        s_w = sem("weights_in")
        s_c = sem("constants_ready")
        s_ctx = sem("context_in")
        s_win = [sem("win0_in"), sem("win1_in")]
        s_x = sem("x_in")
        s_bcw = sem("bc_written")
        s_bcq = [sem(f"bc{q}_in") for q in range(GQ)]
        s_x2w = sem("x2_written")
        s_xfw = [sem("xfT0_written"), sem("xfT1_written")]
        s_in = sem("inproj_done")
        s_xp = sem("xproj_done")
        s_dtm = sem("dtproj_done")
        s_ns = sem("states_summed")
        s_yT = sem("y_transposed")
        s_xfp = sem("xf_transposed")
        s_lgm = sem("logits_done")
        s_halo = sem("halo_ready")
        s_xin = sem("xin_ready")
        s_u = sem("u_ready")
        s_low = sem("xproj_on_chip")
        s_spa = sem("softplus_chain")
        s_sp = sem("softplus_pieces")
        s_dec = sem("decay_ready")
        s_xf = sem("xf_ready")
        s_xfT = sem("xfT_ready")
        s_sz = sem("gate_ready")
        s_ex = sem("router_exp")
        s_cv = sem("conv_taps")
        s_e1 = sem("log1p_rest")
        s_dbu = sem("input_ready")
        s_scan = sem("scan_done")
        s_carry = sem("carry_saved")
        s_y = sem("y_ready")
        s_gate = sem("gated")
        s_stage = [sem(f"stage{i}_in") for i in range(TT)]
        s_ln1 = sem("ln1_steps")
        s_ln1b = sem("ln1_done")
        s_rs1 = sem("ln1_rstd")
        s_cur = sem("ln1_of_row")
        s_zx = sem("gate_in")
        s_bn = sem("ln2_steps")
        s_nb = sem("ln2_bias")
        s_rs2 = sem("ln2_rstd")
        s_sm = sem("softmax_steps")
        s_pc = sem("dt_chain")
        s_dt = sem("dt_ready")
        s_hc = sem("states_times_c")
        s_x2 = sem("x2_ready")
        s_srt = sem("scores_turned")
        s_b = sem("search_step")
        s_cnt = sem("counts_summed")
        s_sel = sem("selection_step")
        s_sp2 = sem("selection_sums")
        s_big = sem("expert_matrix_in")
        s_lx = [sem("xfT_in0"), sem("xfT_in1")]
        s_l2 = [sem("x2_in0"), sem("x2_in1")]
        s_mm = sem("expert_product")
        s_o1 = sem("product_biased")
        s_o = sem("tile_done")
        s_out = [sem("out0_written"), sem("out1_written")]

        block = ctx.enter_context(nc.Block())
        NW = 12

        def state_of(o, g):
            return states[((o % HB) * G + g) % NST]

        stage = [t[:].rearrange("p s t -> p (s t)") for t in (*decay, *states[:2])]
        x_rows = x.rearrange("(b h) t d -> b (h t) d", h=HB)

        def eT(e):
            return slice(e * P, (e + 1) * P)

        ebias = cbc[:, 0:2, :].rearrange("p a t -> p (a t)")
        x2t = [cbc[:, 2 + 2 * i:4 + 2 * i, :].rearrange("p a t -> p (a t)") for i in range(2)]
        ot = [cbc[:, 6 + 2 * i:8 + 2 * i, :].rearrange("p a t -> p (a t)") for i in range(2)]
        wexp = bbc[:].rearrange("p (k a) t -> p k (a t)", k=E)
        srt = decay[0][:, 0, :]
        junk = decay[0][:, 1, :]
        gtm = decay[1][:, 0, :]
        eqm = decay[1][:, 1, :]
        cum = states[0][:, 0, :]
        sele = states[0][:, 1, :]
        ones = states[1][:, 0, :]

        @block.sync
        def _(sp):
            def w(dst, src):
                sp.dma_start(dst, src).then_inc(s_w, 16)

            def load_ctx(b, o):
                sp.dma_start(ctx_sb[:], ctxT[b * HB + o]).then_inc(s_ctx, 16)

            def load_win(b, o, j):
                wait(sp, s_in, n(b, o, E, j - 1))
                sp.dma_start(win[j % 2][:], winT[j]).then_inc(s_win[j % 2], 16)

            def store_x2(b, o):
                wait(sp, s_x2, n(b, o, E, E))
                sp.dma_start(x2_dram[b * HB + o], xt[:]).then_inc(s_x2w, 16)

            def load_gate(b, o):
                wait(sp, s_gate, n(b, o, E, 0))
                h = o % HB
                src = x_rows[b + o // HB].rearrange("(e p) d -> p e d", p=P)[:, :, h * T:(h + 1) * T]
                sp.dma_start(sz[:], src).then_inc(s_zx, 16)

            def load_stage(j):
                wait(sp, s_ln1, 2 * (j - 1) + 1)
                for t in range(TT):
                    k = j * TT + t
                    sp.dma_start(stage[t], x_rows[k // E, (k % E) * P:(k % E + 1) * P, :]).then_inc(s_stage[t], 16)

            def load_x(b, o):
                wait(sp, s_xfp, n(b, o, 2 * TT, 0))
                sp.dma_start(xt[:], x[b * HB + o].rearrange("(t p) d -> p t d", p=P)).then_inc(s_x, 16)

            def store_xfT(b, o, t):
                wait(sp, s_xfT, n(b, o, 2 * TT, 2 * t + 2))
                sp.dma_start(xfT_dram[b * HB + o, t], xfT[t % 2][:].rearrange("p k t -> p (k t)")) \
                    .then_inc(s_xfw[t % 2], 16)

            def store_bc(b, o):
                wait(sp, s_low, n(b, o, 1, 1))
                sp.dma_start(bc_dram[b * HB + o], xpr[R:2 * R, :]).then_inc(s_bcw, 16)
                wait(sp, s_bcw, n(b, o, 16, 16))
                load_ctx(b, o + 1)

            def load_bc(b, o, q):
                wait(sp, s_hc, n(b, o - 1, G, (E - 1) * GQ + q + 1))
                for k, dst in ((0, bbc), (NS, cbc)):
                    src = bc_dram[b * HB + o, k + GN * q:k + GN * (q + 1), :].rearrange("s t -> (s t)")
                    src = src.rearrange("(a f) -> a f", a=1).broadcast_to([P, GN * T])
                    sp.dma_start(dst[:, GN * q:GN * (q + 1), :].rearrange("p s t -> p (s t)"), src) \
                        .then_inc(s_bcq[q], 16)

            def half(b, o, first):
                for j in range(3):
                    load_win(b, o + 1, j)
                load_gate(b, o)
                if not first:
                    store_x2(b, o - 1)
                load_win(b, o + 1, 3)
                load_win(b, o + 1, 4)
                if not first:
                    store_xfT(b, o - 1, 0)
                    store_xfT(b, o - 1, 1)
                load_x(b, o)
                load_win(b, o + 1, 5)
                if not first:
                    store_xfT(b, o - 1, 2)
                    store_xfT(b, o - 1, 3)
                for j in range(6, E):
                    load_win(b, o + 1, j)
                store_bc(b, o + 1)
                for q in range(GQ):
                    load_bc(b, o + 1, q)

            load_ctx(0, 0)
            load_win(0, 0, 0)
            load_win(0, 0, 1)
            w(con[:], consts)
            for dst, src in ((cw, conv_w), (cb, conv_b), (dtb, dt_b), (dv, dvec), (xp, xpT), (dtp, dtpT), (al, a_log),
                             (rw, router_w)):
                w(dst[:], src)
            w(rb[:], router_b.rearrange("(a c s) -> a c s", a=1, c=1).broadcast_to([P, TT, NX]))
            w(gg[:, 0:1], g_xattn.rearrange("(a s) -> a s", a=1).broadcast_to([P, 1]))
            w(gg[:, 1:2], g_ffn.rearrange("(a s) -> a s", a=1).broadcast_to([P, 1]))
            for j in range(E):
                load_stage(j)
                if j >= 2:
                    load_win(0, 0, j)
            store_bc(0, 0)
            for q in range(GQ):
                load_bc(0, 0, q)
            for h in range(HB):
                half(0, h, h == 0)
            with sp.Fori(1, B) as b:
                for h in range(HB):
                    half(b, h, False)
            store_x2(B, -1)
            for t in range(TT):
                store_xfT(B, -1, t)
            for q in range(GQ):
                sp.wait_ge(s_bcq[q], n(B, 0, 32, 32))
            sp.dma_start(wexp, expert_w.rearrange("(k p) f -> p k f", p=P)).then_inc(s_big, 16)
            sp.dma_start(ebias, expert_b.rearrange("(a f) -> a f", a=1).broadcast_to([P, D])).then_inc(s_big, 16)
            sp.wait_ge(s_x2w, n(B, 0, 16, 0))
            for i in range(2):
                sp.wait_ge(s_xfw[i], n(B, 0, 32, 0))
            sp.wait_ge(s_lgm, n(B, 0, TT, 0))

            def load_tile(c, t, k):
                i = t % 2
                wait(sp, s_mm, k - 1)
                sp.dma_start(xfT[i][:].rearrange("p k t -> p (k t)"), xfT_dram[c, t]).then_inc(s_lx[i], 16)
                wait(sp, s_o, k - 1)
                sp.dma_start(x2t[i], x2_dram[c, :, t, :]).then_inc(s_l2[i], 16)

            def store_tile(c, t, k):
                sp.wait_ge(s_o, k + 1)
                sp.dma_start(out[c, t * P:(t + 1) * P, :], ot[t % 2]).then_inc(s_out[t % 2], 16)

            load_tile(0, 0, 0)
            load_tile(0, 1, 1)
            load_tile(0, 2, 2)
            store_tile(0, 0, 0)
            load_tile(0, 3, 3)
            for t in range(1, TT):
                store_tile(0, t, t)
            with sp.Fori(1, NC) as c:
                for t in range(TT):
                    load_tile(c, t, c * TT + t)
                    if t >= 1:
                        store_tile(c, t - 1, c * TT + (t - 1))
                store_tile(c, TT - 1, c * TT + (TT - 1))
            for i in range(2):
                sp.wait_ge(s_out[i], 16 * NC * TT // 2)

        @block.tensor
        def _(pe):
            def inproj(b, o, j):
                wait(pe, s_ctx, n(b, o, 16, 16))
                wait(pe, s_win[j % 2], n(b, o, 16 * E // 2, 16 * (j // 2 + 1)))
                wait(pe, s_xin, n(b, o, E, j - 1))
                if j == 0:
                    wait(pe, s_low, n(b, o, 1, 0))
                for k in range(KC):
                    mm = pe.matmul(pA[j % 2][:], win[j % 2][:, k, :], ctx_sb[:, k, :], start=(k == 0), stop=(k == KC - 1))
                mm.then_inc(s_in, 1)

            def xproj(b, o):
                wait(pe, s_u, n(b, o, 1, 1))
                wait(pe, s_xin, n(b, o, E, E))
                for e in range(E):
                    mm = pe.matmul(pA[0][0:2 * R, :], xp[:, e, :], u[o % 2][:, e, :], start=(e == 0), stop=(e == E - 1))
                mm.then_inc(s_xp, 1)

            def dtproj(b, o, e):
                wait(pe, s_low, n(b, o, 1, 1))
                wait(pe, s_sp, n(b, o, E, e))
                pe.matmul(pD[:], dtp[:, eT(e)], xpr[0:R, :], start=True, stop=True).then_inc(s_dtm, 1)

            def sum_states(b, o, g):
                e = g // GQ
                wait(pe, s_hc, n(b, o, G, g + 1))
                if g % GQ == 0:
                    wait(pe, s_y, n(b, o, E, e - 1))
                for i in range(GN):
                    mm = pe.matmul(pY[e % 2][:], ident, state_of(o, g)[:, i, :],
                                   start=(g % GQ == 0 and i == 0), stop=(g % GQ == GQ - 1 and i == GN - 1))
                mm.then_inc(s_ns, 1)

            def turn_y(b, o, e):
                wait(pe, s_gate, n(b, o, E, e + 1))
                wait(pe, s_x2, n(b, o, E, e))
                for t in range(TT):
                    mm = pe.transpose(pT[:, eT(t)], y[e % 2][:, eT(t)], ident)
                mm.then_inc(s_yT, 1)

            def turn_xf(b, o, f):
                t = f // 2
                wait(pe, s_xf, n(b, o, TT, t + 1))
                wait(pe, s_xfT, n(b, o, 2 * TT, f))
                for k in range(4):
                    mm = pe.transpose(pF[:, eT(k)], xt[:, t, eT(4 * (f % 2) + k)], ident)
                mm.then_inc(s_xfp, 1)

            def logits(b, o, t):
                wait(pe, s_xfT, n(b, o, 2 * TT, 2 * t + 2))
                wait(pe, s_sm, n(b, o - 1, 6, 1))
                for k in range(E):
                    mm = pe.matmul(pL[:, t * NX:(t + 1) * NX], xfT[t % 2][:, k, :], rw[:, k, :], start=(k == 0), stop=(k == E - 1))
                mm.then_inc(s_lgm, 1)

            def half(b, o, first):
                for g in range(G):
                    e, q = divmod(g, GQ)
                    if g in IN_SLOT:
                        inproj(b, o + 1, IN_SLOT.index(g))
                    if g == XP_SLOT:
                        xproj(b, o + 1)
                    if q == 0:
                        dtproj(b, o + (e + 1) // E, (e + 1) % E)
                    if g in YT_SLOT:
                        ye = YT_SLOT.index(g)
                        if ye < E - 1:
                            turn_y(b, o, ye)
                        elif not first:
                            turn_y(b, o - 1, ye)
                    if not first and g in XFP_SLOT:
                        turn_xf(b, o - 1, XFP_SLOT.index(g))
                    if not first and g in LG_SLOT:
                        logits(b, o - 1, LG_SLOT.index(g))
                    sum_states(b, o, g)

            pe.wait_ge(s_w, 16 * NW)
            for j in range(E):
                inproj(0, 0, j)
            xproj(0, 0)
            dtproj(0, 0, 0)
            for h in range(HB):
                half(0, h, h == 0)
            with pe.Fori(1, B) as b:
                for h in range(HB):
                    half(b, h, False)
            turn_y(B, -1, E - 1)
            for t in range(TT):
                turn_xf(B, -1, 2 * t)
                turn_xf(B, -1, 2 * t + 1)
                logits(B, -1, t)
            pe.wait_ge(s_sm, n(B, 0, 6, 0))
            for j in range(TT):
                mm = pe.transpose(pF[:, eT(j)], S_tok[:, j, :, :].rearrange("p c s -> p (c s)"), ident)
            mm.then_inc(s_srt, 1)
            with pe.Fori(0, BITS) as i:
                pe.wait_ge(s_b, i * 4 + (2 + 2))
                pe.matmul(pD[:, 0:1], same_expert, small[:, 0:1], start=True, stop=True).then_inc(s_cnt, 1)
            pe.wait_ge(s_sel, 3)
            pe.matmul(pD[:, 2:3], same_expert, small[:, 1:2], start=True, stop=True)
            pe.matmul(pD[:, 4:5], earlier, cum[:, T - 1:T], start=True, stop=True).then_inc(s_sp2, 1)
            pe.wait_ge(s_sel, 8)
            for j in range(TT):
                mm = pe.matmul(pL[:, j * NC:(j + 1) * NC], sele[:, eT(j)], seg_of, start=True, stop=True)
            mm.then_inc(s_sp2, 1)
            pe.wait_ge(s_big, 32)

            def product(t, k, cc):
                i = t % 2
                pe.wait_ge(s_lx[i], (cc * (TT // 2) + t // 2 + 1) * 16)
                wait(pe, s_o1, k - 1)
                for hh in range(2):
                    for kk in range(E):
                        mm = pe.matmul((pA, pY)[i][hh][:], xfT[i][:, kk, :], wexp[:, kk, hh * 512:(hh + 1) * 512],
                                       start=(kk == 0), stop=(kk == E - 1))
                mm.then_inc(s_mm, 1)

            for t in range(TT):
                product(t, t, 0)
            with pe.Fori(1, NC) as c:
                for t in range(TT):
                    product(t, c * TT + t, c)

        @block.scalar
        def _(act):
            def xin_ready(b, o, j):
                wait(act, s_in, n(b, o, E, j + 1))
                wait(act, s_cv, n(b, o, HALO * E, HALO * (j - 1)))
                if j == 0:
                    wait(act, s_y, n(b, o - 2, E, E))
                first = o % HB == 0
                nc.scalar.copy(xin[j % 2][:, 0:HALO], zero3[:] if first else halo[:, j, :])
                nc.scalar.copy(xin[j % 2][:, HALO:], pA[j % 2][:])
                if first:
                    nc.scalar.copy(halo[:, j, :], pA[j % 2][:, T - HALO:T])
                nc.scalar.activation(u[o % 2][:, j, :], pA[j % 2][:], ACT.Identity, bias=cb[:, j:j + 1],
                                     scale=cw[:, j, HALO:HALO + 1]).then_inc(s_xin, 1)

            def silu_u(b, o):
                wait(act, s_cv, n(b, o, HALO * E, HALO * E))
                uu = u[o % 2][:].rearrange("p e t -> p (e t)")
                nc.scalar.activation(uu, uu, ACT.Silu).then_inc(s_u, 1)

            def low(b, o):
                wait(act, s_xp, n(b, o, 1, 1))
                wait(act, s_dtm, n(b, o, E, 0))
                wait(act, s_bcw, n(b, o, 16, 0))
                nc.scalar.copy(xpr[:], pA[0][0:2 * R, :]).then_inc(s_low, 1)

            def softplus(b, o, e):
                k = n(b, o, 2 * E, 2 * e)
                wait(act, s_dtm, n(b, o, E, e + 1))
                wait(act, s_dt, n(b, o, E, e))
                bias = dtb[:, e:e + 1]
                nc.scalar.activation(sp3[:, 0, :], pD[:], ACT.Abs, bias=bias).then_inc(s_spa, 1)
                act.wait_ge(s_spa, k + 1)
                nc.scalar.activation(sp3[:, 0, :], sp3[:, 0, :], ACT.Exp, scale=-1.0).then_inc(s_spa, 1)
                act.wait_ge(s_spa, k + 2)
                nc.scalar.activation(sp3[:, 1, :], sp3[:, 0, :], ACT.Identity, bias=1.0)
                nc.scalar.activation(sp3[:, 2, :], sp3[:, 0, :], ACT.Ln, bias=1.0)
                nc.scalar.activation(dt[e % 2][:], pD[:], ACT.Relu, bias=bias).then_inc(s_sp, 1)

            def decays(b, o, g):
                e, q = divmod(g, GQ)
                if q == 0:
                    wait(act, s_dt, n(b, o, E, e + 1))
                wait(act, s_scan, n(b, o, G, g - 1))
                for i in range(GN):
                    s = e * NS + q * GN + i
                    a = nc.scalar.activation(decay[g % 2][:, i, :], dt[e % 2][:], ACT.Exp, scale=an[:, s:s + 1])
                a.then_inc(s_dec, 1)

            def norm_x2(b, o):
                wait(act, s_nb, n(b, o, 1, 1))
                wait(act, s_x2w, n(b, o, 16, 16))
                for t in range(TT):
                    nc.scalar.activation(xt[:, t, :], xt[:, t, :], ACT.Identity, bias=nb2[:, t:t + 1],
                                         scale=rs2[:, t:t + 1]).then_inc(s_xf, 1)

            def xfT_out(b, o, f):
                t = f // 2
                wait(act, s_xfp, n(b, o, 2 * TT, f + 1))
                if f % 2 == 0:
                    wait(act, s_lgm, n(b, o, TT, t - 1))
                    wait(act, s_xfw[t % 2], n(b, o, 32, 16 * (t // 2)))
                nc.scalar.copy(xfT[t % 2][:, 4 * (f % 2):4 * (f % 2) + 4, :].rearrange("p k t -> p (k t)"), pF[:]) \
                    .then_inc(s_xfT, 1)

            def gate_silu(b, o):
                wait(act, s_cur, n(b, o, 1, 1))
                wait(act, s_zx, n(b, o, 16, 16))
                for e in range(E):
                    nc.scalar.activation(sz[:, e, :], sz[:, e, :], ACT.Silu, bias=cur[:, 1, e:e + 1],
                                         scale=cur[:, 0, e:e + 1]).then_inc(s_sz, 1)

            def router_exp(b, o):
                wait(act, s_sm, n(b, o, 6, 3))
                nc.scalar.activation(lg[:], lg[:], ACT.Exp).then_inc(s_ex, 1)

            def half(b, o, first):
                for g in range(G):
                    e, q = divmod(g, GQ)
                    decays(b, o, g)
                    if g - 1 in IN_SLOT:
                        xin_ready(b, o + 1, IN_SLOT.index(g - 1))
                    if g == SILU_SLOT:
                        silu_u(b, o + 1)
                    if g == LOW_SLOT:
                        low(b, o + 1)
                    if q == 2:
                        softplus(b, o + (e + 1) // E, (e + 1) % E)
                    if not first:
                        if g == XF_SLOT:
                            norm_x2(b, o - 1)
                        if g - 1 in XFP_SLOT:
                            xfT_out(b, o - 1, XFP_SLOT.index(g - 1))
                        if g == SM_SLOT + 1:
                            router_exp(b, o - 1)
                    if g == SZ_SLOT:
                        gate_silu(b, o)

            act.wait_ge(s_w, 16 * NW)
            nc.scalar.activation(al[:], al[:], ACT.Exp).then_inc(s_c, 1)
            nc.scalar.activation(tg[:], gg[:], ACT.Tanh).then_inc(s_c, 1)
            act.wait_ge(s_c, 5)
            for j in range(E):
                xin_ready(0, 0, j)
            silu_u(0, 0)
            low(0, 0)
            softplus(0, 0, 0)
            for h in range(HB):
                half(0, h, h == 0)
            with act.Fori(1, B) as b:
                for h in range(HB):
                    half(b, h, False)
            norm_x2(B, -1)
            for f in range(2 * TT):
                xfT_out(B, -1, f)
            router_exp(B, -1)

        @block.vector
        def _(dve):
            def conv(b, o, j):
                wait(dve, s_xin, n(b, o, E, j + 1))
                for i in range(HALO):
                    k = n(b, o, HALO * E, HALO * j + i)
                    if i:
                        dve.wait_ge(s_cv, k)
                    nc.vector.scalar_tensor_tensor(out=u[o % 2][:, j, :], in0=xin[j % 2][:, i:i + T],
                                                   scalar=cw[:, j, i:i + 1], in1=u[o % 2][:, j, :],
                                                   op0=ALU.mult, op1=ALU.add).then_inc(s_cv, 1)

            def log1p_rest(b, o, e):
                wait(dve, s_sp, n(b, o, E, e + 1))
                nc.vector.scalar_tensor_tensor(out=sp3[:, 1, :], in0=sp3[:, 1, :], scalar=-1.0, in1=sp3[:, 0, :],
                                               op0=ALU.add, op1=ALU.subtract).then_inc(s_e1, 1)

            def group(b, o, g):
                e, q = divmod(g, GQ)
                if q == 0:
                    wait(dve, s_dt, n(b, o, E, e + 1))
                if e == 0:
                    wait(dve, s_bcq[q], n(b, o, 32, 32))
                assert HB * G % NST == 2
                last = g - NST + 1 + (1 if o % HB == 0 and g < 2 else 0)
                wait(dve, s_ns, n(b, o, G, last))
                st = state_of(o, g)
                nc.vector.tensor_tensor(st[:], dtu[e % 2][:].rearrange("p (a t) -> p a t", a=1).broadcast_to([P, GN, T]),
                                        bbc[:, GN * q:GN * (q + 1), :], ALU.mult).then_inc(s_dbu, 1)
                dve.wait_ge(s_dbu, n(b, o, G, g + 1))
                wait(dve, s_dec, n(b, o, G, g + 1))
                for i in range(GN):
                    s = q * GN + i
                    sc = nc.vector.tensor_tensor_scan(st[:, i, :], decay[g % 2][:, i, :], st[:, i, :],
                                                      0.0 if o % HB == 0 else carry[:, e, s:s + 1],
                                                      ALU.mult, ALU.add)
                sc.then_inc(s_scan, 1)
                if o % HB == 0:
                    dve.wait_ge(s_scan, n(b, o, G, g + 1))
                    nc.vector.tensor_copy(carry[:, e, q * GN:(q + 1) * GN], st[:, :, T - 1]).then_inc(s_carry, 1)

            def y_out(b, o, e):
                wait(dve, s_ns, n(b, o, G, GQ * (e + 1)))
                wait(dve, s_yT, n(b, o, E, e - 1))
                nc.vector.scalar_tensor_tensor(out=y[e % 2][:], in0=u[o % 2][:, e, :], scalar=dv[:, e:e + 1],
                                               in1=pY[e % 2][:], op0=ALU.mult, op1=ALU.add).then_inc(s_y, 1)

            def residual(b, o, e):
                wait(dve, s_yT, n(b, o, E, e + 1))
                if e == 0:
                    wait(dve, s_x, n(b, o, 16, 16))
                nc.vector.scalar_tensor_tensor(out=xt[:, :, eT(e)], in0=pT[:].rearrange("p (t d) -> p t d", t=TT),
                                               scalar=tg[:, 0:1], in1=xt[:, :, eT(e)],
                                               op0=ALU.mult, op1=ALU.add).then_inc(s_x2, 1)

            def ln1_stats(j):
                if j >= 2:
                    dve.wait_ge(s_ln1, 2 * (j - 1))
                for t in range(TT):
                    dve.wait_ge(s_stage[t], 16 * (j + 1))
                    for i in range(2):
                        z = nc.vector.bn_stats(stats[j % 2][:, t, i, :], stage[t][:, i * 512:(i + 1) * 512])
                z.then_inc(s_ln1, 1)
                dve.wait_ge(s_ln1, 2 * j + 1)
                for t in range(TT):
                    k = j * TT + t
                    z = nc.vector.bn_aggr(mv1[:, k // E, k % E, :], stats[j % 2][:, t, :, :].rearrange("p a s -> p (a s)"))
                z.then_inc(s_ln1, 1)

            def row_ln1(b, o):
                wait(dve, s_sz, n(b, o, E, 0))
                nc.vector.tensor_scalar(cur[:], ln1[:, b, :, :], 1.0, None, ALU.mult).then_inc(s_cur, 1)

            def ln2_stats(b, o):
                wait(dve, s_x2, n(b, o, E, E))
                for t in range(TT):
                    for i in range(2):
                        z = nc.vector.bn_stats(stats[0][:, t, i, :], xt[:, t, i * 512:(i + 1) * 512])
                z.then_inc(s_bn, 1)
                dve.wait_ge(s_bn, n(b, o, 3, 1))
                nc.vector.memset(small[:, 15:16], 0.0)
                for t in range(TT):
                    z = nc.vector.bn_aggr(mv2[:, t, :], stats[0][:, t, :, :].rearrange("p a s -> p (a s)"))
                z.then_inc(s_bn, 1)
                dve.wait_ge(s_bn, n(b, o, 3, 2))
                nc.vector.tensor_scalar(ve2[:], mv2[:, :, 1], EPS, None, ALU.add).then_inc(s_bn, 1)

            def ln2_bias(b, o):
                wait(dve, s_rs2, n(b, o, 1, 1))
                nc.vector.scalar_tensor_tensor(out=nb2[:], in0=mv2[:, :, 0], scalar=-1.0, in1=rs2[:],
                                               op0=ALU.mult, op1=ALU.mult).then_inc(s_nb, 1)

            def softmax_in(b, o):
                wait(dve, s_lgm, n(b, o, TT, TT))
                nc.vector.tensor_tensor(lg[:], pL[:, 0:TT * NX].rearrange("p (t s) -> p t s", t=TT), rb[:], ALU.add) \
                    .then_inc(s_sm, 1)
                dve.wait_ge(s_sm, n(b, o, 6, 1))
                nc.vector.tensor_reduce(mx[:], lg[:], AX.X, ALU.max).then_inc(s_sm, 1)
                dve.wait_ge(s_sm, n(b, o, 6, 2))
                nc.vector.tensor_tensor(lg[:], lg[:], mx[:].rearrange("p (t a) -> p t a", a=1).broadcast_to([P, TT, NX]),
                                        ALU.subtract).then_inc(s_sm, 1)

            def softmax_out(b, o):
                wait(dve, s_ex, n(b, o, 1, 1))
                nc.vector.tensor_reduce(sm[:], lg[:], AX.X, ALU.add).then_inc(s_sm, 1)
                dve.wait_ge(s_sm, n(b, o, 6, 4))
                nc.vector.reciprocal(rc[:], sm[:]).then_inc(s_sm, 1)
                dve.wait_ge(s_sm, n(b, o, 6, 5))
                nc.vector.tensor_tensor(S_tok[:, :, b * HB + o, :], lg[:],
                                        rc[:].rearrange("p (t a) -> p t a", a=1).broadcast_to([P, TT, NX]),
                                        ALU.mult).then_inc(s_sm, 1)

            def half(b, o, first):
                for g in range(G):
                    e, q = divmod(g, GQ)
                    group(b, o, g)
                    if g in CONV_SLOT:
                        conv(b, o + 1, CONV_SLOT.index(g))
                    if q == 4:
                        log1p_rest(b, o + (e + 1) // E, (e + 1) % E)
                    if g in Y_SLOT:
                        ye = Y_SLOT.index(g)
                        if ye < E - 1:
                            y_out(b, o, ye)
                        elif not first:
                            y_out(b, o - 1, ye)
                    if g in RES_SLOT:
                        ye = RES_SLOT.index(g)
                        if ye < E - 1:
                            residual(b, o, ye)
                        elif not first:
                            residual(b, o - 1, ye)
                    if not first:
                        if g == LN2_SLOT:
                            ln2_stats(b, o - 1)
                        if g == LN2_SLOT + 2:
                            ln2_bias(b, o - 1)
                        if g == SM_SLOT:
                            softmax_in(b, o - 1)
                        if g == SM_SLOT + 2:
                            softmax_out(b, o - 1)
                    if g == 0:
                        row_ln1(b, o)

            nc.vector.memset(zero3[:], 0.0).then_inc(s_c, 1)
            nc.vector.memset(mhalf[:], -0.5).then_inc(s_c, 1)
            dve.wait_ge(s_w, 16 * NW)
            dve.wait_ge(s_c, 4)
            nc.vector.tensor_scalar(an[:], al[:], -1.0, None, ALU.mult).then_inc(s_c, 1)
            for j in range(E):
                ln1_stats(j)
                conv(0, 0, j)
            dve.wait_ge(s_ln1, 2 * E)
            nc.vector.tensor_scalar(ve1[:], mv1[:, :, :, 1], EPS, None, ALU.add).then_inc(s_ln1b, 1)
            log1p_rest(0, 0, 0)
            dve.wait_ge(s_rs1, 1)
            nc.vector.scalar_tensor_tensor(out=ln1[:, :, 1, :], in0=mv1[:, :, :, 0], scalar=-1.0, in1=ln1[:, :, 0, :],
                                           op0=ALU.mult, op1=ALU.mult).then_inc(s_ln1b, 1)
            dve.wait_ge(s_ln1b, 2)
            for h in range(HB):
                half(0, h, h == 0)
            with dve.Fori(1, B) as b:
                for h in range(HB):
                    half(b, h, False)
            y_out(B, -1, E - 1)
            residual(B, -1, E - 1)
            ln2_stats(B, -1)
            ln2_bias(B, -1)
            softmax_in(B, -1)
            softmax_out(B, -1)

            thr, bit, cand, step = (bits[:, i:i + 1] for i in range(4))
            dve.wait_ge(s_srt, 1)
            dve.wait_ge(s_ns, n(B, 0, G, 0))
            nc.vector.tensor_copy(srt, pF[:]).then_inc(s_b, 1)
            nc.vector.memset(thr, 0)
            nc.vector.memset(ones, 1.0)
            nc.vector.memset(bit, 1 << (BITS - 1)).then_inc(s_b, 1)
            with dve.Fori(0, BITS) as i:
                dve.wait_ge(s_b, i * 4 + 2)
                nc.vector.tensor_tensor(cand, thr, bit, ALU.bitwise_or).then_inc(s_b, 1)
                dve.wait_ge(s_b, i * 4 + 3)
                nc.vector.tensor_scalar(junk, srt, cand.bitcast(F32), 0.0, ALU.is_ge, ALU.add,
                                        accum_out=small[:, 0:1]).then_inc(s_b, 1)
                dve.wait_ge(s_cnt, i + 1)
                nc.vector.scalar_tensor_tensor(out=step, in0=pD[:, 0:1], scalar=float(TOPK), in1=bit,
                                               op0=ALU.is_ge, op1=ALU.mult).then_inc(s_b, 1)
                dve.wait_ge(s_b, i * 4 + 5)
                nc.vector.tensor_scalar(bit, bit, 1, None, ALU.logical_shift_right)
                nc.vector.tensor_tensor(thr, thr, step, ALU.bitwise_or).then_inc(s_b, 1)
            dve.wait_ge(s_b, BITS * 4 + 2)
            thf = thr.bitcast(F32)
            nc.vector.tensor_scalar(gtm, srt, thf, 0.0, ALU.is_gt, ALU.add, accum_out=small[:, 1:2])
            nc.vector.tensor_scalar(eqm, srt, thf, None, ALU.is_equal).then_inc(s_sel, 1)
            dve.wait_ge(s_sel, 1)
            nc.vector.tensor_tensor_scan(cum, ones, eqm, 0.0, ALU.mult, ALU.add).then_inc(s_sel, 2)
            dve.wait_ge(s_sp2, 1)
            nc.vector.tensor_scalar(small[:, 3:4], pD[:, 2:3], -1.0, float(TOPK), ALU.mult, ALU.add).then_inc(s_sel, 1)
            dve.wait_ge(s_sel, 4)
            nc.vector.tensor_tensor(small[:, 4:5], small[:, 3:4], pD[:, 4:5], ALU.subtract).then_inc(s_sel, 1)
            dve.wait_ge(s_sel, 5)
            nc.vector.scalar_tensor_tensor(out=sele, in0=cum, scalar=small[:, 4:5], in1=eqm,
                                           op0=ALU.is_le, op1=ALU.mult).then_inc(s_sel, 1)
            dve.wait_ge(s_sel, 6)
            nc.vector.tensor_tensor(sele, sele, gtm, ALU.add).then_inc(s_sel, 1)
            dve.wait_ge(s_sel, 7)
            nc.vector.tensor_tensor(sele, sele, srt, ALU.mult).then_inc(s_sel, 1)
            dve.wait_ge(s_sp2, 2)
            nc.vector.tensor_scalar(coef[:], pL[:, 0:TT * NC].rearrange("p (t c) -> p t c", t=TT), tg[:, 1:2], None,
                                    ALU.mult).then_inc(s_sel, 1)
            dve.wait_ge(s_sel, 9)
            dve.wait_ge(s_big, 32)

            def finish(t, k, cc, prev_out):
                i = t % 2
                dve.wait_ge(s_mm, k + 1)
                wait(dve, s_out[i], prev_out)
                for hh in range(2):
                    z = nc.vector.tensor_tensor(ot[i][:, hh * 512:(hh + 1) * 512], (pA, pY)[i][hh][:],
                                                ebias[:, hh * 512:(hh + 1) * 512], ALU.add)
                z.then_inc(s_o1, 1)
                dve.wait_ge(s_o1, k + 1)
                dve.wait_ge(s_l2[i], (cc * (TT // 2) + t // 2 + 1) * 16)
                nc.vector.scalar_tensor_tensor(out=ot[i], in0=ot[i], scalar=coef[:, t, cc:cc + 1] if isinstance(cc, int)
                                               else coef[:, t, bass.ds(cc, 1)], in1=x2t[i],
                                               op0=ALU.mult, op1=ALU.add).then_inc(s_o, 1)

            for t in range(TT):
                finish(t, t, 0, 16 * (t // 2))
            with dve.Fori(1, NC) as c:
                for t in range(TT):
                    finish(t, c * TT + t, c, (c * (TT // 2) + t // 2) * 16)

        @block.gpsimd
        def _(pool):
            def dt_block(b, o, e):
                k = n(b, o, 2 * E, 2 * e)
                wait(pool, s_e1, n(b, o, E, e + 1))
                nc.gpsimd.tensor_tensor(sp3[:, 2, :], sp3[:, 2, :], sp3[:, 1, :], ALU.subtract).then_inc(s_pc, 1)
                pool.wait_ge(s_pc, k + 1)
                nc.gpsimd.tensor_tensor(dt[e % 2][:], dt[e % 2][:], sp3[:, 2, :], ALU.add).then_inc(s_pc, 1)
                pool.wait_ge(s_pc, k + 2)
                wait(pool, s_dbu, n(b, o, G, GQ * (e - 1)))
                nc.gpsimd.tensor_tensor(dtu[e % 2][:], dt[e % 2][:], u[o % 2][:, e, :], ALU.mult).then_inc(s_dt, 1)

            def times_c(b, o, g):
                e, q = divmod(g, GQ)
                if e == 0:
                    wait(pool, s_bcq[q], n(b, o, 32, 32))
                if o % HB == 0:
                    wait(pool, s_carry, b * G + (g + 1))
                else:
                    wait(pool, s_scan, n(b, o, G, g + 1))
                st = state_of(o, g)
                nc.gpsimd.tensor_tensor(st[:], st[:], cbc[:, GN * q:GN * (q + 1), :], ALU.mult).then_inc(s_hc, 1)

            def gate(b, o, e):
                wait(pool, s_y, n(b, o, E, e + 1))
                wait(pool, s_sz, n(b, o, E, e + 1))
                nc.gpsimd.tensor_tensor(y[e % 2][:], y[e % 2][:], sz[:, e, :], ALU.mult).then_inc(s_gate, 1)

            def rstd2(b, o):
                wait(pool, s_bn, n(b, o, 3, 3))
                nc.gpsimd.tensor_tensor(rs2[:], ve2[:], mhalf[:, 0, 0:TT], ALU.pow).then_inc(s_rs2, 1)

            def half(b, o, first):
                for g in range(G):
                    e, q = divmod(g, GQ)
                    times_c(b, o, g)
                    if q == 4:
                        dt_block(b, o + (e + 1) // E, (e + 1) % E)
                    if g in Y_SLOT:
                        ye = Y_SLOT.index(g)
                        if ye < E - 1:
                            gate(b, o, ye)
                        elif not first:
                            gate(b, o - 1, ye)
                    if not first and g == LN2_SLOT:
                        rstd2(b, o - 1)

            pool.wait_ge(s_c, 5)
            pool.wait_ge(s_ln1b, 1)
            nc.gpsimd.tensor_tensor(ln1[:, :, 0, :], ve1[:], mhalf[:], ALU.pow).then_inc(s_rs1, 1)
            dt_block(0, 0, 0)
            for h in range(HB):
                half(0, h, h == 0)
            with pool.Fori(1, B) as b:
                for h in range(HB):
                    half(b, h, False)
            gate(B, -1, E - 1)
            rstd2(B, -1)


def _row_masks():
    seg, ex = np.arange(P) // NX, np.arange(P) % NX
    same = ex[:, None] == ex[None, :]
    early = same & (seg[:, None] < seg[None, :])
    of = seg[:, None] == np.arange(NC)[None, :]
    return np.concatenate([np.eye(P), same, early, of], axis=1).astype(np.float32)


def by_block(w):
    return np.moveaxis(w.reshape(E, P, *w.shape[1:]), 0, 1)


def kernel(**inputs):
    import concourse.bacc as _bacc
    from concourse.bass_utils import run_bass_kernel_spmd as _run

    a = {k: np.asarray(v) for k, v in inputs.items()}
    ctx = a["ctx_1024"].reshape(NC, T, KC, P).transpose(0, 3, 2, 1)
    arrays = {
        "x": a["x"].reshape(NC, T, D),
        "ctxT": np.concatenate([ctx, ctx[:2]], axis=0),
        "g_xattn": a["g_xattn"],
        "g_ffn": a["g_ffn"],
        "winT": a["L0_xattn_in_proj_w"].reshape(E, P, KC, P).transpose(0, 3, 2, 1),
        "conv_w": by_block(a["L0_xattn_conv_w"].reshape(D, TAPS)),
        "conv_b": by_block(a["L0_xattn_conv_b"]),
        "xpT": by_block(a["L0_xattn_x_proj_w"].T),
        "dtpT": a["L0_xattn_dt_proj_w"].T,
        "dt_b": by_block(a["L0_xattn_dt_proj_b"]),
        "a_log": by_block(a["L0_xattn_A_log"]).reshape(P, E * NS),
        "dvec": by_block(a["L0_xattn_D"]),
        "router_w": by_block(a["L0_ffn_router_w"]),
        "router_b": a["L0_ffn_router_b"],
        "expert_w": a["L0_ffn_expert_w"],
        "expert_b": a["L0_ffn_expert_b"],
        "consts": _row_masks(),
    }
    arrays = {k: np.ascontiguousarray(v) for k, v in arrays.items()}
    nc = _bacc.Bacc("TRN2", target_bir_lowering=False, num_devices=1)
    args = [nc.dram_tensor(f"in_{k}", v.shape, mybir.dt.from_np(v.dtype), kind="ExternalInput").ap()
            for k, v in arrays.items()]
    o = nc.dram_tensor("out", (NC, T, D), F32, kind="ExternalOutput").ap()
    mamba_moe(nc, *args, o)
    r = _run(nc, [{f"in_{k}": v for k, v in arrays.items()}], core_ids=[0])
    return r.results[0]["out"].reshape(B, L, D)
```

```python
from contextlib import ExitStack

import numpy as np
import concourse.bass as bass
from concourse import mybir

ALU = mybir.AluOpType
ACT = mybir.ActivationFunctionType
AX = mybir.AxisListType
F32 = mybir.dt.float32
U32 = mybir.dt.uint32

P = 128
B, L, D = 4, 1024, 1024
DM = 512
KC = DM // P
E = D // P
NS = 16
R = 32
TAPS = 4
HB = 2
T = L // HB
TT = T // P
NC = B * HB
NX = 16
TOPK = B * L // NX
EPS = 1e-5
GN = 2
GQ = NS // GN
G = E * GQ
NST = 4
BITS = 30
HALO = TAPS - 1

IN_SLOT = [s - G for s in (1, 4, 8, 11, 14, 18, 21, 25)]
XIN_SLOT = [s + 7 for s in IN_SLOT]
CONV_SLOT = [s + 8 for s in IN_SLOT]
SILU_SLOT, XP_SLOT, LOW_SLOT = [37 - G], [s - G for s in (38, 39, 40, 41)], [47 - G]
DTP_SLOT = [GQ * e - 16 for e in range(E)]
SP_SLOT = [GQ * e - 9 for e in range(E)]
REST_SLOT = [s + 1 for s in SP_SLOT]
DT_SLOT = [s + 2 for s in SP_SLOT]
DIAG_SLOT = [GQ * e + 4 for e in range(E)]
SKIP_SLOT = [GQ * e + 7 for e in range(E)]
SZ_SLOT = [9, 41]
Y_SLOT = [s + 4 for s in SKIP_SLOT]
YT_SLOT = [17, 22] + [s + 1 for s in Y_SLOT[2:]]
RES_SLOT = [s + 7 for s in YT_SLOT]
LN2_SLOT = [80 + 14 * t for t in range(TT)]
RS_SLOT = [s + 1 for s in LN2_SLOT]
XF_SLOT = [s + 6 for s in LN2_SLOT]
XFP_SLOT = [s + 7 * f + 1 for s in XF_SLOT for f in range(2)]
XFT_SLOT = [s + 6 for s in XFP_SLOT]
LG_SLOT = [s + 1 for s in XFT_SLOT]
SMI_SLOT, EXP_SLOT, SMO_SLOT = [LG_SLOT[-1] + 4], [LG_SLOT[-1] + 9], [LG_SLOT[-1] + 10]


def at(slots, g, began):
    return [(i, s // G) for i, s in enumerate(slots) if s % G == g and s // G <= began]


def n(b, o, K, k):
    return b * (HB * K) + (o * K + k)


def wait(eng, sem, value):
    if not (isinstance(value, int) and value <= 0):
        eng.wait_ge(sem, value)


def mamba_moe(nc, x, ctxT, g_xattn, g_ffn, winT, conv_w, conv_b, xpT, dtpT, dt_b, a_log, dvec,
              router_w, router_b, expert_w, expert_b, consts, row_masks, out):
    with ExitStack() as ctx:
        def sb(name, shape, dt=F32):
            return ctx.enter_context(nc.sbuf_tensor(name, shape, dt))

        def bank(name):
            return ctx.enter_context(nc.psum_tensor(name, [P, 512], F32))

        def sem(name):
            return ctx.enter_context(nc.semaphore(name))

        bc_dram = nc.dram_tensor("bc_scratch", [NC + 1, 2 * NS, T], F32, kind="Internal").ap()
        x2_dram = nc.dram_tensor("x2_scratch", [NC, P, TT, D], F32, kind="Internal").ap()
        xfT_dram = nc.dram_tensor("xfT_scratch", [NC, TT, P, E * P], F32, kind="Internal").ap()

        win = [sb(f"win{i}", [P, KC, P]) for i in range(2)]
        xp = sb("xp", [P, E, 2 * R])
        dtp = [sb(f"dtp{i}", [R, P]) for i in range(2)]
        cw = sb("cw", [P, E, TAPS])
        cb = sb("cb", [P, E])
        dtb = sb("dtb", [P, E])
        al = sb("al", [P, E * NS])
        an = sb("an", [P, E * NS])
        dv = sb("dv", [P, E])
        rw = sb("rw", [P, E, NX])
        rb = sb("rb", [P, TT, NX])
        gg = sb("gg", [P, 2])
        tg = sb("tg", [P, 2])
        con = sb("con", [P, P])
        ident = con[:]
        tgid = sb("tgid", [P, P])
        ddiag = [sb(f"ddiag{i}", [P, P]) for i in range(2)]
        zero3 = sb("zero3", [P, HALO])
        mhalf = sb("mhalf", [P, B, E])
        ctx_sb = sb("ctx_sb", [P, KC, T])
        xt = sb("xt", [P, TT, D])
        sz = sb("sz", [P, E // 2, T])
        xin = [sb(f"xin{i}", [P, HALO + T]) for i in range(2)]
        halo = sb("halo", [P, E, HALO])
        u = [sb(f"u{i}", [P, E, T]) for i in range(2)]
        sp3 = sb("sp3", [P, 3, T])
        dt = [sb(f"dt{i}", [P, T]) for i in range(2)]
        dtu = [sb(f"dtu{i}", [P, T]) for i in range(2)]
        y = sb("y", [P, T])
        xpr = sb("xpr", [2 * R, T])
        bbc = sb("bbc", [P, NS, T])
        cbc = sb("cbc", [P, NS, T])
        decay = [sb(f"decay{i}", [P, GN, T]) for i in range(NST)]
        states = [sb(f"states{i}", [P, GN, T]) for i in range(NST)]
        carry = sb("carry", [P, E, NS])
        xr = [sb(f"xr{i}", [P, D]) for i in range(2)]
        xfT = sb("xfT", [P, E // 2, P])
        stats = [sb(f"stats{i}", [P, TT, 2, 6]) for i in range(2)]
        mv1 = sb("mv1", [P, B, E, 2])
        ve1 = sb("ve1", [P, B, E])
        ln1 = sb("ln1", [P, B, 2, E])
        cur = sb("cur", [P, 2, E])
        mv2 = sb("mv2", [P, TT, 2])
        ve2 = sb("ve2", [P, TT])
        rs2 = sb("rs2", [P, TT])
        nm2 = sb("nm2", [P, TT])
        nb2 = sb("nb2", [P, TT])
        lg = sb("lg", [P, TT, NX])
        mx = sb("mx", [P, TT])
        sm = sb("sm", [P, TT])
        rc = sb("rc", [P, TT])
        S_tok = sb("S_tok", [P, TT, NC, NX])
        small = sb("small", [P, 16])
        bits = sb("bits", [P, 4], U32)
        coef = sb("coef", [P, TT, NC])

        pA = [bank("pA0"), bank("pA1")]
        pD = bank("pD")
        pY = [bank("pY0"), bank("pY1")]
        pT = bank("pT")
        pF = bank("pF")
        pL = bank("pL")

        s_w = sem("weights_in")
        s_c = sem("constants_ready")
        s_ctx = sem("context_in")
        s_dtp = [sem("dtp0_in"), sem("dtp1_in")]
        s_win = [sem("win0_in"), sem("win1_in")]
        s_x = sem("x_in")
        s_bcw = sem("bc_written")
        s_bcq = [sem(f"bc{q}_in") for q in range(GQ)]
        s_x2w = sem("x2_written")
        s_xfw = sem("xfT_written")
        s_xr = [sem("x2_back0"), sem("x2_back1")]
        s_in = sem("inproj_done")
        s_xp = sem("xproj_done")
        s_dtm = sem("dtproj_done")
        s_ns = sem("states_summed")
        s_yT = sem("y_transposed")
        s_xfp = sem("xf_transposed")
        s_lgm = sem("logits_done")
        s_halo = sem("halo_ready")
        s_xin = sem("xin_ready")
        s_u = sem("u_ready")
        s_low = sem("xproj_on_chip")
        s_spa = sem("softplus_chain")
        s_sp = sem("softplus_pieces")
        s_dec = sem("decay_ready")
        s_xf = sem("xf_ready")
        s_xfT = sem("xfT_ready")
        s_sz = sem("gate_ready")
        s_ex = sem("router_exp")
        s_cv = sem("conv_taps")
        s_e1 = sem("log1p_rest")
        s_dbu = sem("input_ready")
        s_scan = sem("scan_done")
        s_carry = sem("carry_saved")
        s_y = sem("y_ready")
        s_diag = sem("diagonal_ready")
        s_skip = sem("skip_added")
        s_stage = [sem(f"stage{i}_in") for i in range(TT)]
        s_ln1 = sem("ln1_steps")
        s_ln1b = sem("ln1_done")
        s_rs1 = sem("ln1_rstd")
        s_cur = sem("ln1_of_row")
        s_zx = sem("gate_in")
        s_bn = sem("ln2_steps")
        s_rs2 = sem("ln2_rstd")
        s_pr = sem("ln2_pow")
        s_sm = sem("softmax_steps")
        s_pc = sem("dt_chain")
        s_dt = sem("dt_ready")
        s_hc = sem("states_times_c")
        s_x2 = sem("x2_ready")
        s_srt = sem("scores_turned")
        s_b = sem("search_step")
        s_cnt = sem("counts_summed")
        s_sel = sem("selection_step")
        s_sp2 = sem("selection_sums")
        s_mask = sem("masks_in")
        s_big = sem("expert_matrix_in")
        s_lx = [sem(f"xfT_in{t}") for t in range(TT)]
        s_l2 = [sem(f"x2_in{t}") for t in range(TT)]
        s_mm = sem("expert_product")
        s_o1 = sem("product_biased")
        s_o = sem("tile_done")
        s_out = [sem(f"out{t}_written") for t in range(TT)]

        block = ctx.enter_context(nc.Block())
        NW = 11
        EXP_LN = "natural_log_exp_and_others"

        def state_of(o, g):
            return states[g % NST]

        stage = [t[:].rearrange("p s t -> p (s t)") for t in decay]
        x_rows = x.rearrange("(b h) t d -> b (h t) d", h=HB)

        def eT(e):
            return slice(e * P, (e + 1) * P)

        ebias = cbc[:, 0:2, :].rearrange("p a t -> p (a t)")
        masks = cbc[:, 2, 0:2 * P + NC]
        same_expert = masks[:, 0:P]
        earlier = masks[:, P:2 * P]
        seg_of = masks[:, 2 * P:2 * P + NC]
        lt = [sz[:, 2 * i:2 * i + 2, :].rearrange("p a t -> p (a t)") for i in range(2)] + [xr[0][:], xr[1][:]]
        x2t = [xt[:, t, :] for t in range(TT)]
        ot = [u[1][:, 2 * t:2 * t + 2, :].rearrange("p a t -> p (a t)") for t in range(TT)]
        pC = [(pA[0], pA[1]), (pY[0], pY[1]), (pT, pF), (pD, pL)]
        wexp = bbc[:].rearrange("p (k a) t -> p k (a t)", k=E)
        srt = decay[0][:, 0, :]
        junk = decay[0][:, 1, :]
        gtm = decay[1][:, 0, :]
        eqm = decay[1][:, 1, :]
        cum = states[0][:, 0, :]
        sele = states[0][:, 1, :]
        ones = states[1][:, 0, :]

        @block.sync
        def _(sp):
            def w(dst, src):
                sp.dma_start(dst, src).then_inc(s_w, 16)

            def load_ctx(b, o):
                wait(sp, s_in, n(b, o, E, 0))
                sp.dma_start(ctx_sb[:], ctxT[b * HB + o]).then_inc(s_ctx, 16)

            def load_win(b, o, j):
                wait(sp, s_in, n(b, o, E, j - 1))
                sp.dma_start(win[j % 2][:], winT[j]).then_inc(s_win[j % 2], 16)

            def store_x2(b, o):
                wait(sp, s_x2, n(b, o, E, E))
                sp.dma_start(x2_dram[b * HB + o], xt[:]).then_inc(s_x2w, 16)

            def load_dtp(b, o, e):
                wait(sp, s_dtm, n(b, o, E, e - 1))
                sp.dma_start(dtp[e % 2][:], dtpT[e]).then_inc(s_dtp[e % 2], 16)

            def load_gate(b, o, part):
                wait(sp, s_y, n(b, o, E, part * (E // 2)))
                h = o % HB
                src = x_rows[b + o // HB].rearrange("(e p) d -> p e d", p=P)[
                    :, part * (E // 2):(part + 1) * (E // 2), h * T:(h + 1) * T]
                sp.dma_start(sz[:], src).then_inc(s_zx, 16)

            def load_stage(j):
                wait(sp, s_ln1, 2 * (j - 1) + 1)
                for t in range(TT):
                    k = j * TT + t
                    sp.dma_start(stage[t], x_rows[k // E, (k % E) * P:(k % E + 1) * P, :]).then_inc(s_stage[t], 16)

            def load_x(b, o):
                wait(sp, s_x2w, n(b, o, 16, 0))
                sp.dma_start(xt[:], x[b * HB + o].rearrange("(t p) d -> p t d", p=P)).then_inc(s_x, 16)

            def load_xr(b, o, t):
                wait(sp, s_xfp, n(b, o, 2 * TT, 2 * (t - 1)))
                sp.dma_start(xr[t % 2][:], x2_dram[b * HB + o, :, t, :]).then_inc(s_xr[t % 2], 16)

            def store_xfT(b, o, f):
                wait(sp, s_xfT, n(b, o, 2 * TT, f + 1))
                half_of = slice((f % 2) * 512, (f % 2 + 1) * 512)
                sp.dma_start(xfT_dram[b * HB + o, f // 2, :, half_of], xfT[:].rearrange("p k t -> p (k t)")).then_inc(s_xfw, 16)

            def store_bc(b, o):
                wait(sp, s_low, n(b, o, 1, 1))
                sp.dma_start(bc_dram[b * HB + o], xpr[R:2 * R, :]).then_inc(s_bcw, 16)
                wait(sp, s_bcw, n(b, o, 16, 16))

            def load_bc(b, o, q):
                wait(sp, s_hc, n(b, o - 1, G, (E - 1) * GQ + q + 1))
                for k, dst in ((0, bbc), (NS, cbc)):
                    src = bc_dram[b * HB + o, k + GN * q:k + GN * (q + 1), :].rearrange("s t -> (s t)")
                    src = src.rearrange("(a f) -> a f", a=1).broadcast_to([P, GN * T])
                    sp.dma_start(dst[:, GN * q:GN * (q + 1), :].rearrange("p s t -> p (s t)"), src) \
                        .then_inc(s_bcq[q], 16)

            WIN_SLOT = [IN_SLOT[j] - G + 1 for j in (E - 2, E - 1)] + [IN_SLOT[j] + 1 for j in range(E - 2)]
            GATE_SLOT = [s - 6 for s in SZ_SLOT]
            ST_SLOT = [9 + G]
            LX_SLOT = [9]
            XR_SLOT = [9 + G] * 2 + [XFP_SLOT[1] + 1, XFP_SLOT[3] + 1]
            XFW_SLOT = [s + 1 for s in XFT_SLOT]
            CTX_SLOT = [IN_SLOT[-1] - G + 1]
            BC_SLOT = [LOW_SLOT[0] + 1]
            DTW_SLOT = [DTP_SLOT[e] - 15 for e in range(E)]
            BCQ_SLOT = [q - GQ for q in range(GQ)]

            def side(b, o, g, began):
                for i, k in at(WIN_SLOT, g, began):
                    load_win(b, o - k, i)
                for i, k in at(DTW_SLOT, g, began):
                    load_dtp(b, o - k, i)
                for i, k in at(GATE_SLOT, g, began):
                    load_gate(b, o - k, i)
                for i, k in at(ST_SLOT, g, began):
                    store_x2(b, o - k)
                for i, k in at(LX_SLOT, g, began):
                    load_x(b, o - k)
                for i, k in at(XR_SLOT, g, began):
                    load_xr(b, o - k, i)
                for i, k in at(CTX_SLOT, g, began):
                    load_ctx(b, o - k)
                for i, k in at(XFW_SLOT, g, began):
                    store_xfT(b, o - k, i)
                for i, k in at(BC_SLOT, g, began):
                    store_bc(b, o - k)
                for i, k in at(BCQ_SLOT, g, began):
                    load_bc(b, o - k, i)

            def half(b, o, began):
                for g in range(G):
                    side(b, o, g, began)

            load_ctx(0, 0)
            load_win(0, 0, 0)
            load_win(0, 0, 1)
            load_dtp(0, 0, 0)
            load_dtp(0, 0, 1)
            w(con[:], consts)
            for dst, src in ((cw, conv_w), (cb, conv_b), (dtb, dt_b), (dv, dvec), (xp, xpT), (al, a_log),
                             (rw, router_w)):
                w(dst[:], src)
            w(rb[:], router_b.rearrange("(a c s) -> a c s", a=1, c=1).broadcast_to([P, TT, NX]))
            w(gg[:, 0:1], g_xattn.rearrange("(a s) -> a s", a=1).broadcast_to([P, 1]))
            w(gg[:, 1:2], g_ffn.rearrange("(a s) -> a s", a=1).broadcast_to([P, 1]))
            for j in range(E):
                load_stage(j)
                if j >= 2:
                    load_win(0, 0, j)
            store_bc(0, 0)
            load_win(0, 1, 0)
            load_win(0, 1, 1)
            load_ctx(0, 1)
            load_dtp(0, 0, 2)
            load_dtp(0, 0, 3)
            for q in range(GQ):
                load_bc(0, 0, q)
            for h in range(HB):
                half(0, h, h)
            with sp.Fori(1, B) as b:
                for h in range(HB):
                    half(b, h, 2)
            for h in range(HB):
                for g in range(G):
                    for i, k in at(ST_SLOT, g, 2):
                        if k > h:
                            store_x2(B, h - k)
                            sp.wait_ge(s_x2w, n(B, 0, 16, 0))
                    for i, k in at(XR_SLOT, g, 2):
                        if k > h:
                            load_xr(B, h - k, i)
                    for i, k in at(XFW_SLOT, g, 2):
                        if k > h:
                            store_xfT(B, h - k, i)
            for q in range(GQ):
                sp.wait_ge(s_bcq[q], n(B, 0, 32, 32))
            sp.dma_start(wexp, expert_w.rearrange("(k p) f -> p k f", p=P)).then_inc(s_big, 16)
            sp.dma_start(ebias, expert_b.rearrange("(a f) -> a f", a=1).broadcast_to([P, D])).then_inc(s_big, 16)
            sp.dma_start(masks, row_masks).then_inc(s_mask, 16)
            sp.wait_ge(s_x2w, n(B, 0, 16, 0))
            sp.wait_ge(s_xfw, n(B, 0, 16 * 2 * TT, 0))
            sp.wait_ge(s_xfp, n(B, 0, 2 * TT, 0))
            sp.wait_ge(s_y, n(B, 0, E, 0))

            def load_tile(c, t, k):
                wait(sp, s_mm, k - (TT - 1))
                sp.dma_start(lt[t], xfT_dram[c, t]).then_inc(s_lx[t], 16)
                wait(sp, s_o, k - (TT - 1))
                sp.dma_start(x2t[t], x2_dram[c, :, t, :]).then_inc(s_l2[t], 16)

            def store_tile(c, t, k):
                sp.wait_ge(s_o, k + 1)
                sp.dma_start(out[c, t * P:(t + 1) * P, :], ot[t]).then_inc(s_out[t], 16)

            for t in range(TT):
                load_tile(0, t, t)
            with sp.Fori(1, NC) as c:
                for t in range(TT):
                    store_tile(c - 1, t, (c - 1) * TT + t)
                    load_tile(c, t, c * TT + t)
            for t in range(TT):
                store_tile(NC - 1, t, (NC - 1) * TT + t)
            for t in range(TT):
                sp.wait_ge(s_out[t], 16 * NC)

        @block.tensor
        def _(pe):
            def inproj(b, o, j, part):
                ks = range(part * (KC // 2), (part + 1) * (KC // 2))
                if part == 0:
                    inproj_waits(b, o, j)
                for k in ks:
                    mm = pe.matmul(pA[j % 2][:], win[j % 2][:, k, :], ctx_sb[:, k, :], start=(k == 0), stop=(k == KC - 1))
                if part == 1:
                    mm.then_inc(s_in, 1)

            def inproj_waits(b, o, j):
                wait(pe, s_ctx, n(b, o, 16, 16))
                wait(pe, s_win[j % 2], n(b, o, 16 * E // 2, 16 * (j // 2 + 1)))
                wait(pe, s_xin, n(b, o, E, j - 1))
                if j == 0:
                    wait(pe, s_low, n(b, o, 1, 0))

            def xproj(b, o, part):
                if part == 0:
                    wait(pe, s_u, n(b, o, 1, 1))
                    wait(pe, s_xin, n(b, o, E, E))
                for e in range(part * 2, part * 2 + 2):
                    mm = pe.matmul(pA[0][0:2 * R, :], xp[:, e, :], u[o % 2][:, e, :], start=(e == 0), stop=(e == E - 1))
                if part == 3:
                    mm.then_inc(s_xp, 1)

            def dtproj(b, o, e):
                wait(pe, s_low, n(b, o, 1, 1))
                wait(pe, s_dtp[e % 2], n(b, o, 16 * E // 2, 16 * (e // 2 + 1)))
                wait(pe, s_sp, n(b, o, E, e))
                pe.matmul(pD[:], dtp[e % 2][:], xpr[0:R, :], start=True, stop=True).then_inc(s_dtm, 1)

            def sum_states(b, o, g):
                e = g // GQ
                wait(pe, s_hc, n(b, o, G, g + 1))
                if g % GQ == 0:
                    wait(pe, s_y, n(b, o, E, e - 1))
                for i in range(GN):
                    mm = pe.matmul(pY[e % 2][:], ident, state_of(o, g)[:, i, :],
                                   start=(g % GQ == 0 and i == 0), stop=False)
                mm.then_inc(s_ns, 1)

            def add_skip(b, o, e):
                wait(pe, s_diag, n(b, o, E, e + 1))
                pe.matmul(pY[e % 2][:], ddiag[e % 2][:], u[o % 2][:, e, :], start=False, stop=True).then_inc(s_skip, 1)

            def turn_y(b, o, e):
                wait(pe, s_y, n(b, o, E, e + 1))
                wait(pe, s_x2, n(b, o, E, e))
                if e == 0:
                    wait(pe, s_x, n(b, o, 16, 16))
                pe.matmul(pT[:].rearrange("p (t d) -> p t d", t=TT), ident, xt[:, :, eT(e)], start=True, stop=False)
                for t in range(TT):
                    mm = pe.matmul(pT[:, eT(t)], y[:, eT(t)], tgid[:], start=False, stop=(t == TT - 1))
                mm.then_inc(s_yT, 1)

            def turn_xf(b, o, f):
                t = f // 2
                wait(pe, s_xf, n(b, o, TT, t + 1))
                wait(pe, s_xfT, n(b, o, 2 * TT, f))
                for k in range(4):
                    mm = pe.transpose(pF[:, eT(k)], xr[t % 2][:, eT(4 * (f % 2) + k)], ident)
                mm.then_inc(s_xfp, 1)

            def logits(b, o, f):
                t = f // 2
                wait(pe, s_xfT, n(b, o, 2 * TT, f + 1))
                if f == 0:
                    wait(pe, s_sm, n(b, o - 1, 6, 1))
                for k in range(4):
                    mm = pe.matmul(pL[:, t * NX:(t + 1) * NX], xfT[:, k, :], rw[:, 4 * (f % 2) + k, :],
                                   start=(f % 2 == 0 and k == 0), stop=(f % 2 == 1 and k == 3))
                mm.then_inc(s_lgm, 1)

            def side(b, o, g, began):
                for e, k in at(SKIP_SLOT, g, began):
                    add_skip(b, o - k, e)
                for j, k in at(IN_SLOT, g, began):
                    inproj(b, o - k, j, 0)
                for j, k in at([s + 1 for s in IN_SLOT], g, began):
                    inproj(b, o - k, j, 1)
                for i, k in at(XP_SLOT, g, began):
                    xproj(b, o - k, i)
                for e, k in at(DTP_SLOT, g, began):
                    dtproj(b, o - k, e)
                late(b, o, g, began)

            def late(b, o, g, began, least=0):
                for e, k in at(YT_SLOT, g, began):
                    if k >= least:
                        turn_y(b, o - k, e)
                for f, k in at(XFP_SLOT, g, began):
                    if k >= least:
                        turn_xf(b, o - k, f)
                for t, k in at(LG_SLOT, g, began):
                    if k >= least:
                        logits(b, o - k, t)

            def half(b, o, began):
                for g in range(G):
                    sum_states(b, o, g)
                    side(b, o, g, began)

            pe.wait_ge(s_w, 16 * NW)
            pe.wait_ge(s_c, 6)
            for j in range(E):
                inproj(0, 0, j, 0)
                inproj(0, 0, j, 1)
            for i in range(4):
                xproj(0, 0, i)
            dtproj(0, 0, 0)
            dtproj(0, 0, 1)
            for h in range(HB):
                half(0, h, h)
            with pe.Fori(1, B) as b:
                for h in range(HB):
                    half(b, h, 2)
            for h in range(HB):
                for g in range(G):
                    late(B, h, g, 2, h + 1)
            pe.wait_ge(s_sm, n(B, 0, 6, 0))
            pe.wait_ge(s_mask, 16)
            for j in range(TT):
                mm = pe.transpose(pF[:, eT(j)], S_tok[:, j, :, :].rearrange("p c s -> p (c s)"), ident)
            mm.then_inc(s_srt, 1)
            with pe.Fori(0, BITS) as i:
                pe.wait_ge(s_b, i * 4 + (2 + 2))
                pe.matmul(pD[:, 0:1], same_expert, small[:, 0:1], start=True, stop=True).then_inc(s_cnt, 1)
            pe.wait_ge(s_sel, 3)
            pe.matmul(pD[:, 2:3], same_expert, small[:, 1:2], start=True, stop=True)
            pe.matmul(pD[:, 4:5], earlier, cum[:, T - 1:T], start=True, stop=True).then_inc(s_sp2, 1)
            pe.wait_ge(s_sel, 8)
            for j in range(TT):
                mm = pe.matmul(pL[:, j * NC:(j + 1) * NC], sele[:, eT(j)], seg_of, start=True, stop=True)
            mm.then_inc(s_sp2, 1)
            pe.wait_ge(s_big, 32)

            def product(t, k, cc):
                pe.wait_ge(s_lx[t], (cc + 1) * 16)
                wait(pe, s_o1, k - (TT - 1))
                for hh in range(2):
                    for kk in range(E):
                        mm = pe.matmul(pC[t][hh][:], lt[t][:, eT(kk)], wexp[:, kk, hh * 512:(hh + 1) * 512],
                                       start=(kk == 0), stop=(kk == E - 1))
                mm.then_inc(s_mm, 1)

            pe.wait_ge(s_sel, 9)
            for t in range(TT):
                product(t, t, 0)
            with pe.Fori(1, NC) as c:
                for t in range(TT):
                    product(t, c * TT + t, c)

        @block.scalar
        def _(act):
            def xin_ready(b, o, j):
                wait(act, s_in, n(b, o, E, j + 1))
                wait(act, s_cv, n(b, o, HALO * E, HALO * (j - 1)))
                if j == 0:
                    wait(act, s_skip, n(b, o - 2, E, E))
                first = o % HB == 0
                nc.scalar.copy(xin[j % 2][:, 0:HALO], zero3[:] if first else halo[:, j, :])
                nc.scalar.copy(xin[j % 2][:, HALO:], pA[j % 2][:])
                if first:
                    nc.scalar.copy(halo[:, j, :], pA[j % 2][:, T - HALO:T])
                nc.scalar.activation(u[o % 2][:, j, :], pA[j % 2][:], ACT.Identity, bias=cb[:, j:j + 1],
                                     scale=cw[:, j, HALO:HALO + 1]).then_inc(s_xin, 1)

            def silu_u(b, o):
                wait(act, s_cv, n(b, o, HALO * E, HALO * E))
                uu = u[o % 2][:].rearrange("p e t -> p (e t)")
                nc.scalar.activation(uu, uu, ACT.Silu).then_inc(s_u, 1)
                nc.scalar.preload_act_table_set(EXP_LN)

            def low(b, o):
                wait(act, s_xp, n(b, o, 1, 1))
                wait(act, s_dtm, n(b, o, E, 0))
                wait(act, s_bcw, n(b, o, 16, 0))
                nc.scalar.copy(xpr[:], pA[0][0:2 * R, :]).then_inc(s_low, 1)

            def softplus(b, o, e):
                k = n(b, o, 2 * E, 2 * e)
                wait(act, s_dtm, n(b, o, E, e + 1))
                wait(act, s_dt, n(b, o, E, e))
                bias = dtb[:, e:e + 1]
                nc.scalar.activation(sp3[:, 0, :], pD[:], ACT.Abs, bias=bias).then_inc(s_spa, 1)
                act.wait_ge(s_spa, k + 1)
                nc.scalar.activation(sp3[:, 0, :], sp3[:, 0, :], ACT.Exp, scale=-1.0).then_inc(s_spa, 1)
                act.wait_ge(s_spa, k + 2)
                nc.scalar.activation(sp3[:, 1, :], sp3[:, 0, :], ACT.Identity, bias=1.0)
                nc.scalar.activation(sp3[:, 2, :], sp3[:, 0, :], ACT.Ln, bias=1.0)
                nc.scalar.activation(dt[e % 2][:], pD[:], ACT.Relu, bias=bias).then_inc(s_sp, 1)

            def decays(b, o, g):
                e, q = divmod(g, GQ)
                if q == 0:
                    wait(act, s_dt, n(b, o, E, e + 1))
                wait(act, s_scan, n(b, o, G, g - (NST - 1)))
                for i in range(GN):
                    s = e * NS + q * GN + i
                    a = nc.scalar.activation(decay[g % NST][:, i, :], dt[e % 2][:], ACT.Exp, scale=an[:, s:s + 1])
                a.then_inc(s_dec, 1)

            def diagonal(b, o, e):
                wait(act, s_skip, n(b, o, E, e - 1))
                nc.scalar.activation(ddiag[e % 2][:], ident, ACT.Copy, scale=dv[:, e:e + 1]).then_inc(s_diag, 1)

            def residual(b, o, e):
                wait(act, s_yT, n(b, o, E, e + 1))
                nc.scalar.copy(xt[:, :, eT(e)], pT[:].rearrange("p (t d) -> p t d", t=TT)).then_inc(s_x2, 1)

            def norm_x2(b, o, t):
                wait(act, s_rs2, n(b, o, TT, t + 1))
                nc.scalar.activation(xr[t % 2][:], xr[t % 2][:], ACT.Identity, bias=nb2[:, t:t + 1],
                                     scale=rs2[:, t:t + 1]).then_inc(s_xf, 1)

            def xfT_out(b, o, f):
                t = f // 2
                wait(act, s_xfp, n(b, o, 2 * TT, f + 1))
                wait(act, s_lgm, n(b, o, 2 * TT, f))
                wait(act, s_xfw, n(b, o, 16 * 2 * TT, 16 * f))
                nc.scalar.copy(xfT[:].rearrange("p k t -> p (k t)"), pF[:]) \
                    .then_inc(s_xfT, 1)

            def gate_silu(b, o, part):
                if part == 0:
                    wait(act, s_cur, n(b, o, 1, 1))
                wait(act, s_zx, n(b, o, 32, 16 * (part + 1)))
                for i in range(E // 2):
                    e = part * (E // 2) + i
                    nc.scalar.activation(sz[:, i, :], sz[:, i, :], ACT.Silu, bias=cur[:, 1, e:e + 1],
                                         scale=cur[:, 0, e:e + 1]).then_inc(s_sz, 1)
                nc.scalar.preload_act_table_set(EXP_LN)

            def router_exp(b, o):
                wait(act, s_sm, n(b, o, 6, 3))
                nc.scalar.activation(lg[:], lg[:], ACT.Exp).then_inc(s_ex, 1)

            def late(b, o, g, began, least=0):
                for e, k in at(RES_SLOT, g, began):
                    if k >= least:
                        residual(b, o - k, e)
                for f, k in at(XFT_SLOT, g, began):
                    if k >= least:
                        xfT_out(b, o - k, f)
                for t, k in at(XF_SLOT, g, began):
                    if k >= least:
                        norm_x2(b, o - k, t)
                for _, k in at(EXP_SLOT, g, began):
                    if k >= least:
                        router_exp(b, o - k)

            def half(b, o, began):
                for g in range(G):
                    decays(b, o, g)
                    for e, k in at(DIAG_SLOT, g, began):
                        diagonal(b, o - k, e)
                    for j, k in at(XIN_SLOT, g, began):
                        xin_ready(b, o - k, j)
                    for _, k in at(SILU_SLOT, g, began):
                        silu_u(b, o - k)
                    for _, k in at(LOW_SLOT, g, began):
                        low(b, o - k)
                    for e, k in at(SP_SLOT, g, began):
                        softplus(b, o - k, e)
                    for part, k in at(SZ_SLOT, g, began):
                        gate_silu(b, o - k, part)
                    late(b, o, g, began)

            act.wait_ge(s_w, 16 * NW)
            nc.scalar.activation(al[:], al[:], ACT.Exp).then_inc(s_c, 1)
            nc.scalar.activation(tg[:], gg[:], ACT.Tanh).then_inc(s_c, 1)
            nc.scalar.preload_act_table_set(EXP_LN)
            act.wait_ge(s_c, 6)
            for j in range(E):
                xin_ready(0, 0, j)
            silu_u(0, 0)
            low(0, 0)
            softplus(0, 0, 0)
            softplus(0, 0, 1)
            for h in range(HB):
                half(0, h, h)
            with act.Fori(1, B) as b:
                for h in range(HB):
                    half(b, h, 2)
            for h in range(HB):
                for g in range(G):
                    late(B, h, g, 2, h + 1)

        @block.vector
        def _(dve):
            def conv(b, o, j):
                wait(dve, s_xin, n(b, o, E, j + 1))
                for i in range(HALO):
                    k = n(b, o, HALO * E, HALO * j + i)
                    if i:
                        dve.wait_ge(s_cv, k)
                    nc.vector.scalar_tensor_tensor(out=u[o % 2][:, j, :], in0=xin[j % 2][:, i:i + T],
                                                   scalar=cw[:, j, i:i + 1], in1=u[o % 2][:, j, :],
                                                   op0=ALU.mult, op1=ALU.add).then_inc(s_cv, 1)

            def log1p_rest(b, o, e):
                wait(dve, s_sp, n(b, o, E, e + 1))
                nc.vector.scalar_tensor_tensor(out=sp3[:, 1, :], in0=sp3[:, 1, :], scalar=-1.0, in1=sp3[:, 0, :],
                                               op0=ALU.add, op1=ALU.subtract).then_inc(s_e1, 1)

            def input_of(b, o, g, i):
                e, q = divmod(g, GQ)
                if i == 0:
                    if q == 0:
                        wait(dve, s_dt, n(b, o, E, e + 1))
                    if e == 0:
                        wait(dve, s_bcq[q], n(b, o, 32, 32))
                    wait(dve, s_ns, n(b, o, G, g - (NST - 1)))
                nc.vector.tensor_tensor(state_of(o, g)[:, i, :], dtu[e % 2][:], bbc[:, GN * q + i, :], ALU.mult) \
                    .then_inc(s_dbu, 1)

            def keep_carry(b, o, g):
                e, q = divmod(g, GQ)
                dve.wait_ge(s_scan, n(b, o, G, g + 1))
                nc.vector.tensor_copy(carry[:, e, q * GN:(q + 1) * GN], state_of(o, g)[:, :, T - 1]).then_inc(s_carry, 1)

            def group(b, o, g):
                e, q = divmod(g, GQ)
                input_of(b, o, g, 0)
                if g and o % HB == 0:
                    keep_carry(b, o, g - 1)
                elif g == 0 and o % HB == 1:
                    keep_carry(b, o - 1, G - 1)
                for i in range(1, GN):
                    input_of(b, o, g, i)
                st = state_of(o, g)
                for i in range(GN):
                    dve.wait_ge(s_dbu, n(b, o, GN * G, GN * g + i + 1))
                    if i == 0:
                        wait(dve, s_dec, n(b, o, G, g + 1))
                    s = q * GN + i
                    sc = nc.vector.tensor_tensor_scan(st[:, i, :], decay[g % NST][:, i, :], st[:, i, :],
                                                      0.0 if o % HB == 0 else carry[:, e, s:s + 1],
                                                      ALU.mult, ALU.add)
                sc.then_inc(s_scan, 1)

            def y_out(b, o, e):
                wait(dve, s_skip, n(b, o, E, e + 1))
                wait(dve, s_sz, n(b, o, E, e + 1))
                wait(dve, s_yT, n(b, o, E, e))
                nc.vector.tensor_tensor(y[:], pY[e % 2][:], sz[:, e % (E // 2), :], ALU.mult).then_inc(s_y, 1)

            def ln1_stats(j):
                if j >= 2:
                    dve.wait_ge(s_ln1, 2 * (j - 1))
                for t in range(TT):
                    dve.wait_ge(s_stage[t], 16 * (j + 1))
                    for i in range(2):
                        z = nc.vector.bn_stats(stats[j % 2][:, t, i, :], stage[t][:, i * 512:(i + 1) * 512])
                z.then_inc(s_ln1, 1)
                dve.wait_ge(s_ln1, 2 * j + 1)
                for t in range(TT):
                    k = j * TT + t
                    z = nc.vector.bn_aggr(mv1[:, k // E, k % E, :], stats[j % 2][:, t, :, :].rearrange("p a s -> p (a s)"))
                z.then_inc(s_ln1, 1)

            def row_ln1(b, o):
                wait(dve, s_sz, n(b, o, E, 0))
                nc.vector.tensor_scalar(cur[:], ln1[:, b, :, :], 1.0, None, ALU.mult).then_inc(s_cur, 1)

            def ln2_stats(b, o, t):
                k = n(b, o, 3 * TT, 3 * t)
                wait(dve, s_xr[t % 2], n(b, o, 16 * TT // 2, 16 * (t // 2 + 1)))
                for i in range(2):
                    z = nc.vector.bn_stats(stats[0][:, t, i, :], xr[t % 2][:, i * 512:(i + 1) * 512])
                z.then_inc(s_bn, 1)
                dve.wait_ge(s_bn, k + 1)
                nc.vector.memset(small[:, 15:16], 0.0)
                nc.vector.bn_aggr(mv2[:, t, :], stats[0][:, t, :, :].rearrange("p a s -> p (a s)")).then_inc(s_bn, 1)
                dve.wait_ge(s_bn, k + 2)
                nc.vector.tensor_scalar(nm2[:, t:t + 1], mv2[:, t, 0:1], -1.0, None, ALU.mult)
                nc.vector.tensor_scalar(ve2[:, t:t + 1], mv2[:, t, 1:2], EPS, None, ALU.add).then_inc(s_bn, 1)

            def softmax_in(b, o):
                wait(dve, s_lgm, n(b, o, 2 * TT, 2 * TT))
                nc.vector.tensor_tensor(lg[:], pL[:, 0:TT * NX].rearrange("p (t s) -> p t s", t=TT), rb[:], ALU.add) \
                    .then_inc(s_sm, 1)
                dve.wait_ge(s_sm, n(b, o, 6, 1))
                nc.vector.tensor_reduce(mx[:], lg[:], AX.X, ALU.max).then_inc(s_sm, 1)
                dve.wait_ge(s_sm, n(b, o, 6, 2))
                nc.vector.tensor_tensor(lg[:], lg[:], mx[:].rearrange("p (t a) -> p t a", a=1).broadcast_to([P, TT, NX]),
                                        ALU.subtract).then_inc(s_sm, 1)

            def softmax_out(b, o):
                wait(dve, s_ex, n(b, o, 1, 1))
                nc.vector.tensor_reduce(sm[:], lg[:], AX.X, ALU.add).then_inc(s_sm, 1)
                dve.wait_ge(s_sm, n(b, o, 6, 4))
                nc.vector.reciprocal(rc[:], sm[:]).then_inc(s_sm, 1)
                dve.wait_ge(s_sm, n(b, o, 6, 5))
                nc.vector.tensor_tensor(S_tok[:, :, b * HB + o, :], lg[:],
                                        rc[:].rearrange("p (t a) -> p t a", a=1).broadcast_to([P, TT, NX]),
                                        ALU.mult).then_inc(s_sm, 1)

            def late(b, o, g, began, least=0):
                for e, k in at(Y_SLOT, g, began):
                    if k >= least:
                        y_out(b, o - k, e)
                for t, k in at(LN2_SLOT, g, began):
                    if k >= least:
                        ln2_stats(b, o - k, t)
                for _, k in at(SMI_SLOT, g, began):
                    if k >= least:
                        softmax_in(b, o - k)
                for _, k in at(SMO_SLOT, g, began):
                    if k >= least:
                        softmax_out(b, o - k)

            def half(b, o, began):
                for g in range(G):
                    group(b, o, g)
                    for j, k in at(CONV_SLOT, g, began):
                        conv(b, o - k, j)
                    for e, k in at(REST_SLOT, g, began):
                        log1p_rest(b, o - k, e)
                    late(b, o, g, began)
                    if g == 4:
                        row_ln1(b, o)

            nc.vector.memset(zero3[:], 0.0).then_inc(s_c, 1)
            nc.vector.memset(mhalf[:], -0.5).then_inc(s_c, 1)
            dve.wait_ge(s_w, 16 * NW)
            dve.wait_ge(s_c, 4)
            nc.vector.tensor_scalar(an[:], al[:], -1.0, None, ALU.mult).then_inc(s_c, 1)
            nc.vector.tensor_scalar(tgid[:], ident, tg[:, 0:1], None, ALU.mult).then_inc(s_c, 1)
            for j in range(E):
                ln1_stats(j)
                conv(0, 0, j)
            dve.wait_ge(s_ln1, 2 * E)
            nc.vector.tensor_scalar(ve1[:], mv1[:, :, :, 1], EPS, None, ALU.add).then_inc(s_ln1b, 1)
            log1p_rest(0, 0, 0)
            dve.wait_ge(s_rs1, 1)
            nc.vector.scalar_tensor_tensor(out=ln1[:, :, 1, :], in0=mv1[:, :, :, 0], scalar=-1.0, in1=ln1[:, :, 0, :],
                                           op0=ALU.mult, op1=ALU.mult).then_inc(s_ln1b, 1)
            dve.wait_ge(s_ln1b, 2)
            for h in range(HB):
                half(0, h, h)
            with dve.Fori(1, B) as b:
                for h in range(HB):
                    half(b, h, 2)
            for h in range(HB):
                for g in range(G):
                    late(B, h, g, 2, h + 1)

            thr, bit, cand, step = (bits[:, i:i + 1] for i in range(4))
            dve.wait_ge(s_srt, 1)
            dve.wait_ge(s_ns, n(B, 0, G, 0))
            nc.vector.tensor_copy(srt, pF[:]).then_inc(s_b, 1)
            nc.vector.memset(thr, 0)
            nc.vector.memset(ones, 1.0)
            nc.vector.memset(bit, 1 << (BITS - 1)).then_inc(s_b, 1)
            with dve.Fori(0, BITS) as i:
                dve.wait_ge(s_b, i * 4 + 2)
                nc.vector.tensor_tensor(cand, thr, bit, ALU.bitwise_or).then_inc(s_b, 1)
                dve.wait_ge(s_b, i * 4 + 3)
                nc.vector.tensor_scalar(junk, srt, cand.bitcast(F32), 0.0, ALU.is_ge, ALU.add,
                                        accum_out=small[:, 0:1]).then_inc(s_b, 1)
                dve.wait_ge(s_cnt, i + 1)
                nc.vector.scalar_tensor_tensor(out=step, in0=pD[:, 0:1], scalar=float(TOPK), in1=bit,
                                               op0=ALU.is_ge, op1=ALU.mult).then_inc(s_b, 1)
                dve.wait_ge(s_b, i * 4 + 5)
                nc.vector.tensor_scalar(bit, bit, 1, None, ALU.logical_shift_right)
                nc.vector.tensor_tensor(thr, thr, step, ALU.bitwise_or).then_inc(s_b, 1)
            dve.wait_ge(s_b, BITS * 4 + 2)
            thf = thr.bitcast(F32)
            nc.vector.tensor_scalar(gtm, srt, thf, 0.0, ALU.is_gt, ALU.add, accum_out=small[:, 1:2])
            nc.vector.tensor_scalar(eqm, srt, thf, None, ALU.is_equal).then_inc(s_sel, 1)
            dve.wait_ge(s_sel, 1)
            nc.vector.tensor_tensor_scan(cum, ones, eqm, 0.0, ALU.mult, ALU.add).then_inc(s_sel, 2)
            dve.wait_ge(s_sp2, 1)
            nc.vector.tensor_scalar(small[:, 3:4], pD[:, 2:3], -1.0, float(TOPK), ALU.mult, ALU.add).then_inc(s_sel, 1)
            dve.wait_ge(s_sel, 4)
            nc.vector.tensor_tensor(small[:, 4:5], small[:, 3:4], pD[:, 4:5], ALU.subtract).then_inc(s_sel, 1)
            dve.wait_ge(s_sel, 5)
            nc.vector.scalar_tensor_tensor(out=sele, in0=cum, scalar=small[:, 4:5], in1=eqm,
                                           op0=ALU.is_le, op1=ALU.mult).then_inc(s_sel, 1)
            dve.wait_ge(s_sel, 6)
            nc.vector.tensor_tensor(sele, sele, gtm, ALU.add).then_inc(s_sel, 1)
            dve.wait_ge(s_sel, 7)
            nc.vector.tensor_tensor(sele, sele, srt, ALU.mult).then_inc(s_sel, 1)
            dve.wait_ge(s_sp2, 2)
            nc.vector.tensor_scalar(coef[:], pL[:, 0:TT * NC].rearrange("p (t c) -> p t c", t=TT), tg[:, 1:2], None,
                                    ALU.mult).then_inc(s_sel, 1)
            dve.wait_ge(s_sel, 9)
            dve.wait_ge(s_big, 32)

            def finish(t, k, cc):
                dve.wait_ge(s_mm, k + 1)
                wait(dve, s_out[t], cc * 16)
                for hh in range(2):
                    z = nc.vector.tensor_tensor(ot[t][:, hh * 512:(hh + 1) * 512], pC[t][hh][:],
                                                ebias[:, hh * 512:(hh + 1) * 512], ALU.add)
                z.then_inc(s_o1, 1)
                dve.wait_ge(s_o1, k + 1)
                dve.wait_ge(s_l2[t], (cc + 1) * 16)
                nc.vector.scalar_tensor_tensor(out=ot[t], in0=ot[t], scalar=coef[:, t, cc:cc + 1] if isinstance(cc, int)
                                               else coef[:, t, bass.ds(cc, 1)], in1=x2t[t],
                                               op0=ALU.mult, op1=ALU.add).then_inc(s_o, 1)

            for t in range(TT):
                finish(t, t, 0)
            with dve.Fori(1, NC) as c:
                for t in range(TT):
                    finish(t, c * TT + t, c)

        @block.gpsimd
        def _(pool):
            def dt_block(b, o, e):
                k = n(b, o, 2 * E, 2 * e)
                wait(pool, s_e1, n(b, o, E, e + 1))
                nc.gpsimd.tensor_tensor(sp3[:, 2, :], sp3[:, 2, :], sp3[:, 1, :], ALU.subtract).then_inc(s_pc, 1)
                pool.wait_ge(s_pc, k + 1)
                nc.gpsimd.tensor_tensor(dt[e % 2][:], dt[e % 2][:], sp3[:, 2, :], ALU.add).then_inc(s_pc, 1)
                pool.wait_ge(s_pc, k + 2)
                wait(pool, s_dbu, n(b, o, GN * G, GN * GQ * (e - 1)))
                nc.gpsimd.tensor_tensor(dtu[e % 2][:], dt[e % 2][:], u[o % 2][:, e, :], ALU.mult).then_inc(s_dt, 1)

            def times_c(b, o, g):
                e, q = divmod(g, GQ)
                if e == 0:
                    wait(pool, s_bcq[q], n(b, o, 32, 32))
                if o % HB == 0:
                    wait(pool, s_carry, b * G + (g + 1))
                else:
                    wait(pool, s_scan, n(b, o, G, g + 1))
                st = state_of(o, g)
                nc.gpsimd.tensor_tensor(st[:], st[:], cbc[:, GN * q:GN * (q + 1), :], ALU.mult).then_inc(s_hc, 1)

            def rstd2(b, o, t):
                wait(pool, s_bn, n(b, o, 3 * TT, 3 * t + 3))
                nc.gpsimd.tensor_tensor(rs2[:, t:t + 1], ve2[:, t:t + 1], mhalf[:, 0, 0:1], ALU.pow).then_inc(s_pr, 1)
                pool.wait_ge(s_pr, n(b, o, TT, t + 1))
                nc.gpsimd.tensor_tensor(nb2[:, t:t + 1], nm2[:, t:t + 1], rs2[:, t:t + 1], ALU.mult).then_inc(s_rs2, 1)

            def late(b, o, g, began, least=0):
                for t, k in at(RS_SLOT, g, began):
                    if k >= least:
                        rstd2(b, o - k, t)

            def half(b, o, began):
                for g in range(G):
                    times_c(b, o, g)
                    for e, k in at(DT_SLOT, g, began):
                        dt_block(b, o - k, e)
                    late(b, o, g, began)

            pool.wait_ge(s_c, 5)
            pool.wait_ge(s_ln1b, 1)
            nc.gpsimd.tensor_tensor(ln1[:, :, 0, :], ve1[:], mhalf[:], ALU.pow).then_inc(s_rs1, 1)
            dt_block(0, 0, 0)
            for h in range(HB):
                half(0, h, h)
            with pool.Fori(1, B) as b:
                for h in range(HB):
                    half(b, h, 2)
            for h in range(HB):
                for g in range(G):
                    late(B, h, g, 2, h + 1)


def _row_masks():
    seg, ex = np.arange(P) // NX, np.arange(P) % NX
    same = ex[:, None] == ex[None, :]
    early = same & (seg[:, None] < seg[None, :])
    of = seg[:, None] == np.arange(NC)[None, :]
    return np.concatenate([same, early, of], axis=1).astype(np.float32)


def by_block(w):
    return np.moveaxis(w.reshape(E, P, *w.shape[1:]), 0, 1)


def kernel(**inputs):
    import concourse.bacc as _bacc
    from concourse.bass_utils import run_bass_kernel_spmd as _run

    a = {k: np.asarray(v) for k, v in inputs.items()}
    ctx = a["ctx_1024"].reshape(NC, T, KC, P).transpose(0, 3, 2, 1)
    arrays = {
        "x": a["x"].reshape(NC, T, D),
        "ctxT": np.concatenate([ctx, ctx[:2]], axis=0),
        "g_xattn": a["g_xattn"],
        "g_ffn": a["g_ffn"],
        "winT": a["L0_xattn_in_proj_w"].reshape(E, P, KC, P).transpose(0, 3, 2, 1),
        "conv_w": by_block(a["L0_xattn_conv_w"].reshape(D, TAPS)),
        "conv_b": by_block(a["L0_xattn_conv_b"]),
        "xpT": by_block(a["L0_xattn_x_proj_w"].T),
        "dtpT": a["L0_xattn_dt_proj_w"].reshape(E, P, R).transpose(0, 2, 1),
        "dt_b": by_block(a["L0_xattn_dt_proj_b"]),
        "a_log": by_block(a["L0_xattn_A_log"]).reshape(P, E * NS),
        "dvec": by_block(a["L0_xattn_D"]),
        "router_w": by_block(a["L0_ffn_router_w"]),
        "router_b": a["L0_ffn_router_b"],
        "expert_w": a["L0_ffn_expert_w"],
        "expert_b": a["L0_ffn_expert_b"],
        "consts": np.eye(P, dtype=np.float32),
        "row_masks": _row_masks(),
    }
    arrays = {k: np.ascontiguousarray(v) for k, v in arrays.items()}
    nc = _bacc.Bacc("TRN2", target_bir_lowering=False, num_devices=1)
    args = [nc.dram_tensor(f"in_{k}", v.shape, mybir.dt.from_np(v.dtype), kind="ExternalInput").ap()
            for k, v in arrays.items()]
    o = nc.dram_tensor("out", (NC, T, D), F32, kind="ExternalOutput").ap()
    mamba_moe(nc, *args, o)
    r = _run(nc, [{f"in_{k}": v for k, v in arrays.items()}], core_ids=[0])
    return r.results[0]["out"].reshape(B, L, D)
```

```python
from contextlib import ExitStack

import numpy as np
import concourse.bass as bass
from concourse import mybir

ALU = mybir.AluOpType
ACT = mybir.ActivationFunctionType
AX = mybir.AxisListType
F32 = mybir.dt.float32
U32 = mybir.dt.uint32
F32R = mybir.dt.float32r

P = 128
B, L, D = 4, 1024, 1024
DM = 512
KC = DM // P
E = D // P
NS = 16
R = 32
TAPS = 4
HB = 2
T = L // HB
TT = T // P
NC = B * HB
NX = 16
TOPK = B * L // NX
EPS = 1e-5
GN = 2
GQ = NS // GN
G = E * GQ
NST = 4
AHEAD = 5
BITS = 30
HALO = TAPS - 1
LOW_BITS = 12

IN_SLOT = [s - G for s in (0, 4, 9, 13, 17, 20, 23, 26)]
XIN_SLOT = [s + 8 for s in IN_SLOT]
CONV_SLOT = [s + 9 for s in IN_SLOT]
SILU_SLOT, XP_SLOT, LOW_SLOT = [40 - G], [s - G for s in (41, 42, 43, 44)], [50 - G]
DTP_SLOT = [-14] + [GQ * e - 16 for e in range(1, E)]
SP_SLOT = [GQ * e - 9 for e in range(E)]
REST_SLOT = [SP_SLOT[0] + 1] + [s - 1 for s in SP_SLOT[1:]]
DT_SLOT = [SP_SLOT[0] + 1] + SP_SLOT[1:]
DIAG_SLOT = [GQ * e + 4 for e in range(E)]
SKIP_SLOT = [GQ * e + 7 for e in range(E)]
SZ_SLOT = [10, 45]
Y_SLOT = [12, 23] + [s + (8 if s == 39 else 5) for s in SKIP_SLOT[2:]]
YT_SLOT = [18, 24] + [s + 1 for s in Y_SLOT[2:]]
RES_SLOT = [s + 7 for s in YT_SLOT]
LN2_SLOT = [84 + 14 * t for t in range(TT)]
RS_SLOT = [s + 1 for s in LN2_SLOT]
XF_SLOT = [s + 6 for s in LN2_SLOT]
XFP_SLOT = [s + 7 * f + 1 for s in XF_SLOT for f in range(2)]
XFT_SLOT = [s + 6 for s in XFP_SLOT]
LG_SLOT = [s + 1 for s in XFT_SLOT]
SMI_SLOT, EXP_SLOT, SMO_SLOT = [LG_SLOT[-1] + 4], [LG_SLOT[-1] + 9], [LG_SLOT[-1] + 10]


def at(slots, g, began):
    return [(i, s // G) for i, s in enumerate(slots) if s % G == g and s // G <= began]


def n(b, o, K, k):
    return b * (HB * K) + (o * K + k)


def wait(eng, sem, value):
    if not (isinstance(value, int) and value <= 0):
        eng.wait_ge(sem, value)


def mamba_moe(nc, x, ctxT, g_xattn, g_ffn, winT, conv_w, conv_b, xpT, dtpT, dt_b, a_log, dvec,
              router_w, router_b, expert_w, expert_b, consts, row_masks, out):
    with ExitStack() as ctx:
        def sb(name, shape, dt=F32):
            return ctx.enter_context(nc.sbuf_tensor(name, shape, dt))

        def bank(name):
            return ctx.enter_context(nc.psum_tensor(name, [P, 512], F32))

        def sem(name):
            return ctx.enter_context(nc.semaphore(name))

        bc_dram = nc.dram_tensor("bc_scratch", [NC + 1, 2 * NS, T], F32, kind="Internal").ap()
        x2_dram = nc.dram_tensor("x2_scratch", [NC, P, TT, D], F32, kind="Internal").ap()
        xfT_dram = nc.dram_tensor("xfT_scratch", [NC, TT, P, E * P], F32, kind="Internal").ap()

        win = [sb(f"win{i}", [P, KC, P]) for i in range(2)]
        xp = sb("xp", [P, E, 2 * R])
        dtp = [sb(f"dtp{i}", [R, P]) for i in range(2)]
        cw = sb("cw", [P, E, TAPS])
        cb = sb("cb", [P, E])
        dtb = sb("dtb", [P, E])
        al = sb("al", [P, E * NS])
        an = sb("an", [P, E * NS])
        dv = sb("dv", [P, E])
        rw = sb("rw", [P, E, NX])
        rb = sb("rb", [P, TT, NX])
        gg = sb("gg", [P, 2])
        tg = sb("tg", [P, 2])
        con = sb("con", [P, P])
        ident = con[:]
        tgid = sb("tgid", [P, P])
        ddiag = [sb(f"ddiag{i}", [P, P]) for i in range(2)]
        zero3 = sb("zero3", [P, HALO])
        mhalf = sb("mhalf", [P, B, E])
        ctx_sb = sb("ctx_sb", [P, KC, T])
        xt = sb("xt", [P, TT, D])
        sz = sb("sz", [P, E // 2, T])
        xin = [sb(f"xin{i}", [P, HALO + T]) for i in range(2)]
        halo = sb("halo", [P, E, HALO])
        u = [sb(f"u{i}", [P, E, T]) for i in range(2)]
        sp3 = sb("sp3", [P, 3, T])
        dt = [sb(f"dt{i}", [P, T]) for i in range(2)]
        dtu = [sb(f"dtu{i}", [P, T]) for i in range(2)]
        y = sb("y", [P, T])
        xpr = sb("xpr", [2 * R, T])
        decay = [sb(f"decay{i}", [P, GN, T]) for i in range(2)]
        states = [sb(f"states{i}", [P, GN, T]) for i in range(2)]
        carry = sb("carry", [P, E, NS])
        xr = [sb(f"xr{i}", [P, D]) for i in range(2)]
        xfT = sb("xfT", [P, E // 2, P])
        stats = [sb(f"stats{i}", [P, TT, 2, 6]) for i in range(2)]
        mv1 = sb("mv1", [P, B, E, 2])
        ve1 = sb("ve1", [P, B, E])
        ln1 = sb("ln1", [P, B, 2, E])
        cur = sb("cur", [P, 2, E])
        mv2 = sb("mv2", [P, TT, 2])
        ve2 = sb("ve2", [P, TT])
        rs2 = sb("rs2", [P, TT])
        nm2 = sb("nm2", [P, TT])
        nb2 = sb("nb2", [P, TT])
        lg = sb("lg", [P, TT, NX])
        mx = sb("mx", [P, TT])
        sm = sb("sm", [P, TT])
        rc = sb("rc", [P, TT])
        S_tok = sb("S_tok", [P, TT, NC, NX])
        small = sb("small", [P, 16])
        bits = sb("bits", [P, 4], U32)
        coef = sb("coef", [P, TT, NC])
        with ExitStack() as scan:
            def scan_sb(name, shape):
                return scan.enter_context(nc.sbuf_tensor(name, shape, F32))

            bbc = scan_sb("bbc", [P, NS, T])
            cbc = scan_sb("cbc", [P, NS, T])
            decay += [scan_sb(f"decay{i}", [P, GN, T]) for i in range(2, NST)]
            states += [scan_sb(f"states{i}", [P, GN, T]) for i in range(2, NST)]
        whi = sb("whi", [P, E, D], F32R)
        wlo = sb("wlo", [P, E, D], F32R)
        thi = [sb(f"thi{i}", [P, D], F32R) for i in range(2)]
        tlo = [sb(f"tlo{i}", [P, D], F32R) for i in range(2)]

        pA = [bank("pA0"), bank("pA1")]
        pD = bank("pD")
        pY = [bank("pY0"), bank("pY1")]
        pT = bank("pT")
        pF = bank("pF")
        pL = bank("pL")

        s_w = sem("weights_in")
        s_c = sem("constants_ready")
        s_ctx = sem("context_in")
        s_dtp = [sem("dtp0_in"), sem("dtp1_in")]
        s_win = [sem("win0_in"), sem("win1_in")]
        s_x = sem("x_in")
        s_bcw = sem("bc_written")
        s_bcq = [sem(f"bc{q}_in") for q in range(GQ)]
        s_x2w = sem("x2_written")
        s_xfw = sem("xfT_written")
        s_xr = [sem("x2_back0"), sem("x2_back1")]
        s_in = sem("inproj_done")
        s_xp = sem("xproj_done")
        s_dtm = sem("dtproj_done")
        s_ns = sem("states_summed")
        s_yT = sem("y_transposed")
        s_xfp = sem("xf_transposed")
        s_lgm = sem("logits_done")
        s_xin = sem("xin_ready")
        s_u = sem("u_ready")
        s_low = sem("xproj_on_chip")
        s_spa = sem("softplus_chain")
        s_sp = sem("softplus_pieces")
        s_dec = sem("decay_ready")
        s_xf = sem("xf_ready")
        s_xfT = sem("xfT_ready")
        s_sz = sem("gate_ready")
        s_ex = sem("router_exp")
        s_cv = sem("conv_taps")
        s_e1 = sem("log1p_rest")
        s_dbu = sem("input_ready")
        s_scan = sem("scan_done")
        s_carry = sem("carry_saved")
        s_y = sem("y_ready")
        s_diag = sem("diagonal_ready")
        s_skip = sem("skip_added")
        s_stage = [sem(f"stage{j}_in") for j in range(E)]
        s_ln1 = sem("ln1_steps")
        s_ln1b = sem("ln1_done")
        s_rs1 = sem("ln1_rstd")
        s_cur = sem("ln1_of_row")
        s_zx = sem("gate_in")
        s_bn = sem("ln2_steps")
        s_rs2 = sem("ln2_rstd")
        s_pr = sem("ln2_pow")
        s_sm = sem("softmax_steps")
        s_pc = sem("dt_chain")
        s_dt = sem("dt_ready")
        s_hc = sem("states_times_c")
        s_x2 = sem("x2_ready")
        s_srt = sem("scores_turned")
        s_b = sem("search_step")
        s_cnt = sem("counts_summed")
        s_sel = sem("selection_step")
        s_sp2 = sem("selection_sums")
        s_mask = sem("masks_in")
        s_big = sem("expert_bias_in")
        s_wr = [sem(f"expert_rows{i}_in") for i in range(4)]
        s_cut = sem("cut")
        s_hi = sem("high_half")
        s_lo = sem("low_half")
        s_lx = [sem(f"xfT_in{t}") for t in range(TT)]
        s_l2 = [sem(f"x2_in{t}") for t in range(TT)]
        s_mm = sem("expert_product")
        s_ev = sem("product_on_chip")
        s_o1 = sem("product_biased")
        s_o = sem("tile_done")
        s_out = [sem(f"out{t}_written") for t in range(TT)]

        block = ctx.enter_context(nc.Block())
        NW = 11
        EXP_LN = "natural_log_exp_and_others"

        def state_of(o, g):
            return states[g % NST]

        def tiles_of(t):
            return [t[:, 2 * i:2 * i + 2, :].rearrange("p s t -> p (s t)") for i in range(t.shape[1] // 2)]

        stage = [x for t in (*decay, *states, cbc, sz, bbc) for x in tiles_of(t)]
        stage += [xt[:, t, :] for t in range(TT)] + [xr[0][:], xr[1][:]]
        x_rows = x.rearrange("(b h) t d -> b (h t) d", h=HB)

        def eT(e):
            return slice(e * P, (e + 1) * P)

        wraw = [u[0][:, 2 * i:2 * i + 2, :].rearrange("p a t -> p (a t)") for i in range(4)]
        ebias = sp3[:, 0:2, :].rearrange("p a t -> p (a t)")
        masks = sp3[:, 2, 0:2 * P + NC]
        same_expert = masks[:, 0:P]
        earlier = masks[:, P:2 * P]
        seg_of = masks[:, 2 * P:2 * P + NC]
        cut = [ctx_sb[:, 2 * i:2 * i + 2, :].rearrange("p a t -> p (a t)") for i in range(2)]
        lt = [sz[:, 2 * i:2 * i + 2, :].rearrange("p a t -> p (a t)") for i in range(2)] + [xr[0][:], xr[1][:]]
        x2t = [xt[:, t, :] for t in range(TT)]
        ot = [u[1][:, 2 * t:2 * t + 2, :].rearrange("p a t -> p (a t)") for t in range(TT)]
        pC = [pA, pY]
        srt = decay[0][:, 0, :]
        junk = decay[0][:, 1, :]
        gtm = decay[1][:, 0, :]
        eqm = decay[1][:, 1, :]
        cum = states[0][:, 0, :]
        sele = states[0][:, 1, :]
        ones = states[1][:, 0, :]

        @block.sync
        def _(sp):
            def w(dst, src):
                sp.dma_start(dst, src).then_inc(s_w, 16)

            def load_ctx(b, o):
                wait(sp, s_in, n(b, o, E, 0))
                sp.dma_start(ctx_sb[:], ctxT[b * HB + o]).then_inc(s_ctx, 16)

            def load_win(b, o, j):
                wait(sp, s_in, n(b, o, E, j - 1))
                sp.dma_start(win[j % 2][:], winT[j]).then_inc(s_win[j % 2], 16)

            def store_x2(b, o):
                wait(sp, s_x2, n(b, o, E, E))
                sp.dma_start(x2_dram[b * HB + o], xt[:]).then_inc(s_x2w, 16)

            def load_dtp(b, o, e):
                wait(sp, s_dtm, n(b, o, E, e - 1))
                sp.dma_start(dtp[e % 2][:], dtpT[e]).then_inc(s_dtp[e % 2], 16)

            def load_gate(b, o, part):
                wait(sp, s_y, n(b, o, E, part * (E // 2)))
                h = o % HB
                src = x_rows[b + o // HB].rearrange("(e p) d -> p e d", p=P)[
                    :, part * (E // 2):(part + 1) * (E // 2), h * T:(h + 1) * T]
                sp.dma_start(sz[:], src).then_inc(s_zx, 16)

            def load_stage(j, part):
                for t in range(part * 2, part * 2 + 2):
                    k = j * TT + t
                    sp.dma_start(stage[k], x_rows[k // E, (k % E) * P:(k % E + 1) * P, :]).then_inc(s_stage[j], 16)

            def load_x(b, o):
                sp.dma_start(xt[:], x[b * HB + o].rearrange("(t p) d -> p t d", p=P)).then_inc(s_x, 16)

            def load_xr(b, o, t):
                if t == 0:
                    wait(sp, s_x2w, n(b, o, 16, 16))
                else:
                    wait(sp, s_xfp, n(b, o, 2 * TT, 2 * (t - 1)))
                sp.dma_start(xr[t % 2][:], x2_dram[b * HB + o, :, t, :]).then_inc(s_xr[t % 2], 16)

            def store_xfT(b, o, f, src=None):
                src = xfT[:].rearrange("p k t -> p (k t)") if src is None else src
                wait(sp, s_xfT, n(b, o, 2 * TT, f + 1))
                half_of = slice((f % 2) * 512, (f % 2 + 1) * 512)
                sp.dma_start(xfT_dram[b * HB + o, f // 2, :, half_of], src).then_inc(s_xfw, 16)

            def store_bc(b, o):
                wait(sp, s_low, n(b, o, 1, 1))
                sp.dma_start(bc_dram[b * HB + o], xpr[R:2 * R, :]).then_inc(s_bcw, 16)
                wait(sp, s_bcw, n(b, o, 16, 16))

            def load_bc(b, o, q):
                wait(sp, s_hc, n(b, o - 1, G, (E - 1) * GQ + q + 1))
                for k, dst in ((0, bbc), (NS, cbc)):
                    src = bc_dram[b * HB + o, k + GN * q:k + GN * (q + 1), :].rearrange("s t -> (s t)")
                    src = src.rearrange("(a f) -> a f", a=1).broadcast_to([P, GN * T])
                    sp.dma_start(dst[:, GN * q:GN * (q + 1), :].rearrange("p s t -> p (s t)"), src) \
                        .then_inc(s_bcq[q], 16)

            WIN_SLOT = [IN_SLOT[j] - G + 5 for j in (E - 2, E - 1)] + [IN_SLOT[j] + 5 for j in range(E - 2)]
            GATE_SLOT = [4, 38]
            ST_SLOT = [9 + G]
            LX_SLOT = [9]
            XR_SLOT = [9 + G, 13 + G] + [XFP_SLOT[1] + 1, XFP_SLOT[3] + 1]
            XFW_SLOT = [s + 1 for s in XFT_SLOT]
            CTX_SLOT = [IN_SLOT[-1] - G + 5]
            BC_SLOT = [LOW_SLOT[0] + 1]
            DTW_SLOT = [DTP_SLOT[e] - 15 for e in range(E)]
            BCQ_SLOT = [q - GQ for q in range(GQ)]

            def side(b, o, g, began):
                for i, k in at(WIN_SLOT, g, began):
                    load_win(b, o - k, i)
                for i, k in at(DTW_SLOT, g, began):
                    load_dtp(b, o - k, i)
                for i, k in at(GATE_SLOT, g, began):
                    load_gate(b, o - k, i)
                for i, k in at(ST_SLOT, g, began):
                    store_x2(b, o - k)
                for i, k in at(XR_SLOT, g, began):
                    load_xr(b, o - k, i)
                for i, k in at(LX_SLOT, g, began):
                    load_x(b, o - k)
                for i, k in at(CTX_SLOT, g, began):
                    load_ctx(b, o - k)
                for i, k in at(XFW_SLOT, g, began):
                    store_xfT(b, o - k, i)
                for i, k in at(BC_SLOT, g, began):
                    store_bc(b, o - k)
                for i, k in at(BCQ_SLOT, g, began):
                    load_bc(b, o - k, i)

            def half(b, o, began):
                for g in range(G):
                    side(b, o, g, began)

            load_ctx(0, 0)
            load_win(0, 0, 0)
            load_win(0, 0, 1)
            load_dtp(0, 0, 0)
            load_dtp(0, 0, 1)
            w(con[:], consts)
            for dst, src in ((cw, conv_w), (cb, conv_b), (dtb, dt_b), (dv, dvec), (xp, xpT), (al, a_log),
                             (rw, router_w)):
                w(dst[:], src)
            w(rb[:], router_b.rearrange("(a c s) -> a c s", a=1, c=1).broadcast_to([P, TT, NX]))
            w(gg[:, 0:1], g_xattn.rearrange("(a s) -> a s", a=1).broadcast_to([P, 1]))
            w(gg[:, 1:2], g_ffn.rearrange("(a s) -> a s", a=1).broadcast_to([P, 1]))
            for k in range(2 * E):
                if 2 <= k < E:
                    load_win(0, 0, k)
                load_stage(k // 2, k % 2)
            load_win(0, 1, 0)
            load_win(0, 1, 1)
            load_ctx(0, 1)
            store_bc(0, 0)
            load_dtp(0, 0, 2)
            load_dtp(0, 0, 3)
            sp.wait_ge(s_ln1, 2 * E)
            for q in range(GQ):
                load_bc(0, 0, q)
            for h in range(HB):
                half(0, h, h)
            with sp.Fori(1, B) as b:
                for h in range(HB):
                    half(b, h, 2)

            def load_w(k):
                wait(sp, s_lo, k - 3)
                sp.dma_start(wraw[k % 4], expert_w[k * P:(k + 1) * P, :]).then_inc(s_wr[k % 4], 16)

            tiles_left = [f for f in range(2 * TT) if XFW_SLOT[f] >= 2 * G]
            for f in tiles_left[:-1]:
                store_xfT(B, -2, f)
            sp.wait_ge(s_dt, n(B, 0, E, 1))
            sp.wait_ge(s_sp, n(B, 0, E, 2))
            for q in range(GQ):
                sp.wait_ge(s_bcq[q], n(B, 0, 32, 32))
            for k in range(4):
                load_w(k)
            store_xfT(B, -2, tiles_left[-1])
            store_x2(B, -1)
            for t in range(TT):
                store_xfT(B, -1, 2 * t, u[1][:, 2 * t, :])
                store_xfT(B, -1, 2 * t + 1, u[1][:, 2 * t + 1, :])
                if t < TT - 2:
                    load_w(2 * t + 4)
                    load_w(2 * t + 5)
            sp.dma_start(ebias, expert_b.rearrange("(a f) -> a f", a=1).broadcast_to([P, D])).then_inc(s_big, 16)
            sp.dma_start(masks, row_masks).then_inc(s_mask, 16)
            sp.wait_ge(s_x2w, n(B, 0, 16, 0))
            sp.wait_ge(s_xfw, n(B, 0, 16 * 2 * TT, 0))
            sp.wait_ge(s_xfp, n(B, 0, 2 * TT, 0))
            sp.wait_ge(s_y, n(B, 0, E, 0))

            def load_lt(c, t, k, first=False):
                if not first:
                    sp.wait_ge(s_lo, k + (E - TT + 1))
                sp.dma_start(lt[t], xfT_dram[c, t]).then_inc(s_lx[t], 16)

            def load_x2t(c, t, k, first=False):
                if not first:
                    sp.wait_ge(s_o, k - (TT - 1))
                sp.dma_start(x2t[t], x2_dram[c, :, t, :]).then_inc(s_l2[t], 16)

            def store_tile(c, t, k):
                sp.wait_ge(s_o, k + 1)
                sp.dma_start(out[c, t * P:(t + 1) * P, :], ot[t]).then_inc(s_out[t], 16)

            for t in range(TT):
                load_lt(0, t, t, True)
            for t in range(TT):
                load_x2t(0, t, t, True)
            for t in range(TT - 1):
                load_lt(1, t, TT + t)

            def step(c, t, more=True):
                k = c * TT + t
                store_tile(c - 1, t, k - TT)
                load_x2t(c, t, k)
                if t == 0:
                    load_lt(c, TT - 1, k + (TT - 1))
                elif more:
                    load_lt(c + 1, t - 1, k + (TT - 1))

            with sp.Fori(1, NC - 1) as c:
                for t in range(TT):
                    step(c, t)
            for t in range(TT):
                step(NC - 1, t, False)
            for t in range(TT):
                store_tile(NC - 1, t, (NC - 1) * TT + t)
            for t in range(TT):
                sp.wait_ge(s_out[t], 16 * NC)

        @block.tensor
        def _(pe):
            def inproj(b, o, j, part):
                if part == 0:
                    inproj_waits(b, o, j)
                mm = pe.matmul(pA[j % 2][:], win[j % 2][:, part, :], ctx_sb[:, part, :],
                               start=(part == 0), stop=(part == KC - 1))
                if part == KC - 1:
                    mm.then_inc(s_in, 1)

            def inproj_waits(b, o, j):
                wait(pe, s_ctx, n(b, o, 16, 16))
                wait(pe, s_win[j % 2], n(b, o, 16 * E // 2, 16 * (j // 2 + 1)))
                wait(pe, s_xin, n(b, o, E, j - 1))
                if j == 0:
                    wait(pe, s_low, n(b, o, 1, 0))

            def xproj(b, o, part):
                if part == 0:
                    wait(pe, s_u, n(b, o, 1, 1))
                    wait(pe, s_xin, n(b, o, E, E))
                for e in range(part * 2, part * 2 + 2):
                    mm = pe.matmul(pA[0][0:2 * R, :], xp[:, e, :], u[o % 2][:, e, :], start=(e == 0), stop=(e == E - 1))
                if part == 3:
                    mm.then_inc(s_xp, 1)

            def dtproj(b, o, e):
                wait(pe, s_low, n(b, o, 1, 1))
                wait(pe, s_dtp[e % 2], n(b, o, 16 * E // 2, 16 * (e // 2 + 1)))
                wait(pe, s_sp, n(b, o, E, e))
                pe.matmul(pD[:], dtp[e % 2][:], xpr[0:R, :], start=True, stop=True).then_inc(s_dtm, 1)

            def sum_states(b, o, g):
                e = g // GQ
                wait(pe, s_hc, n(b, o, G, g + 1))
                if g % GQ == 0:
                    wait(pe, s_y, n(b, o, E, e - 1))
                for i in range(GN):
                    mm = pe.matmul(pY[e % 2][:], ident, state_of(o, g)[:, i, :],
                                   start=(g % GQ == 0 and i == 0), stop=False)
                    mm.then_inc(s_ns, 1)

            def add_skip(b, o, e):
                wait(pe, s_diag, n(b, o, E, e + 1))
                pe.matmul(pY[e % 2][:], ddiag[e % 2][:], u[o % 2][:, e, :], start=False, stop=True).then_inc(s_skip, 1)

            def turn_y(b, o, e):
                wait(pe, s_y, n(b, o, E, e + 1))
                wait(pe, s_x2, n(b, o, E, e))
                if e == 0:
                    wait(pe, s_x, n(b, o, 16, 16))
                pe.matmul(pT[:].rearrange("p (t d) -> p t d", t=TT), ident, xt[:, :, eT(e)], start=True, stop=False)
                for t in range(TT):
                    mm = pe.matmul(pT[:, eT(t)], y[:, eT(t)], tgid[:], start=False, stop=(t == TT - 1))
                mm.then_inc(s_yT, 1)

            def turn_xf(b, o, f, last=False):
                t = f // 2
                wait(pe, s_xf, n(b, o, TT, t + 1))
                wait(pe, s_xfT, n(b, o, 2 * TT, max(f - 1, 0) if last else f))
                for k in range(4):
                    mm = pe.transpose((pT if last and f % 2 else pF)[:, eT(k)], xr[t % 2][:, eT(4 * (f % 2) + k)], ident)
                mm.then_inc(s_xfp, 1)

            def logits(b, o, f, last=False):
                t = f // 2
                piece = u[1][:, f, :].rearrange("p (k t) -> p k t", k=4) if last else xfT[:]
                wait(pe, s_xfT, n(b, o, 2 * TT, f + 1))
                if f == 0:
                    wait(pe, s_sm, n(b, o - 1, 6, 1))
                for k in range(4):
                    mm = pe.matmul(pL[:, t * NX:(t + 1) * NX], piece[:, k, :], rw[:, 4 * (f % 2) + k, :],
                                   start=(f % 2 == 0 and k == 0), stop=(f % 2 == 1 and k == 3))
                mm.then_inc(s_lgm, 1)

            def side(b, o, g, began):
                for e, k in at(SKIP_SLOT, g, began):
                    add_skip(b, o - k, e)
                for part in range(KC):
                    for j, k in at([s + part for s in IN_SLOT], g, began):
                        inproj(b, o - k, j, part)
                for i, k in at(XP_SLOT, g, began):
                    xproj(b, o - k, i)
                for e, k in at(DTP_SLOT, g, began):
                    dtproj(b, o - k, e)
                late(b, o, g, began)

            def late(b, o, g, began, least=0):
                for e, k in at(YT_SLOT, g, began):
                    if k >= least:
                        turn_y(b, o - k, e)
                for f, k in at(XFP_SLOT, g, began):
                    if k >= least:
                        turn_xf(b, o - k, f, k == least)
                for t, k in at(LG_SLOT, g, began):
                    if k >= least:
                        logits(b, o - k, t, k == least)

            def half(b, o, began):
                for g in range(G):
                    sum_states(b, o, g)
                    side(b, o, g, began)

            pe.wait_ge(s_w, 16 * NW)
            pe.wait_ge(s_c, 6)
            for j in range(E):
                for part in range(KC):
                    inproj(0, 0, j, part)
            for i in range(4):
                xproj(0, 0, i)
            dtproj(0, 0, 0)
            dtproj(0, 0, 1)
            for h in range(HB):
                half(0, h, h)
            with pe.Fori(1, B) as b:
                for h in range(HB):
                    half(b, h, 2)
            for h in range(HB):
                for g in range(G):
                    late(B, h, g, 2, h + 1)
            pe.wait_ge(s_sm, n(B, 0, 6, 0))
            pe.wait_ge(s_mask, 16)
            for j in range(TT):
                mm = pe.transpose(pF[:, eT(j)], S_tok[:, j, :, :].rearrange("p c s -> p (c s)"), ident)
            mm.then_inc(s_srt, 1)

            def product_rows(t, k, kk, parts=(0, 1, 2)):
                if kk == 0 and parts[0] == 0:
                    pe.wait_ge(s_hi, k + (E + 1))
                    pe.wait_ge(s_lo, k + (E + 1))
                    wait(pe, s_ev, k - 1)
                hi, lo = thi[t % 2], tlo[t % 2]
                for part in parts:
                    x_part, w_part = ((hi, whi), (hi, wlo), (lo, whi))[part]
                    for hh in range(2):
                        mm = pe.matmul(pC[t % 2][hh][:], x_part[:, eT(kk)],
                                       w_part[:, kk, hh * 512:(hh + 1) * 512],
                                       start=(kk == 0 and part == 0), stop=(kk == E - 1 and part == 2))
                if kk == E - 1 and parts[-1] == 2:
                    mm.then_inc(s_mm, 1)

            rows = [(k, kk, part) for k in range(AHEAD) for kk in range(E) for part in range(3)]
            for i in range(BITS):
                pe.wait_ge(s_b, i * 4 + (2 + 2))
                pe.matmul(pD[:, 0:1], same_expert, small[:, 0:1], start=True, stop=True).then_inc(s_cnt, 1)
                for k, kk, part in rows[i * len(rows) // BITS:(i + 1) * len(rows) // BITS]:
                    product_rows(k % TT, k, kk, (part,))
            pe.wait_ge(s_sel, 3)
            pe.matmul(pD[:, 2:3], same_expert, small[:, 1:2], start=True, stop=True)
            pe.matmul(pD[:, 4:5], earlier, cum[:, T - 1:T], start=True, stop=True).then_inc(s_sp2, 1)
            pe.wait_ge(s_sel, 8)
            for j in range(TT):
                mm = pe.matmul(pL[:, j * NC:(j + 1) * NC], sele[:, eT(j)], seg_of, start=True, stop=True)
            mm.then_inc(s_sp2, 1)
            for k in range(AHEAD, 2 * TT):
                for kk in range(E):
                    product_rows(k % TT, k, kk)
            with pe.Fori(2, NC) as c:
                for t in range(TT):
                    for kk in range(E):
                        product_rows(t, c * TT + t, kk)

        @block.scalar
        def _(act):
            def xin_ready(b, o, j):
                wait(act, s_in, n(b, o, E, j + 1))
                wait(act, s_cv, n(b, o, HALO * E, HALO * (j - 1)))
                if j == 0:
                    wait(act, s_skip, n(b, o - 2, E, E))
                first = o % HB == 0
                nc.scalar.copy(xin[j % 2][:, 0:HALO], zero3[:] if first else halo[:, j, :])
                nc.scalar.copy(xin[j % 2][:, HALO:], pA[j % 2][:])
                if first:
                    nc.scalar.copy(halo[:, j, :], pA[j % 2][:, T - HALO:T])
                nc.scalar.activation(u[o % 2][:, j, :], pA[j % 2][:], ACT.Identity, bias=cb[:, j:j + 1],
                                     scale=cw[:, j, HALO:HALO + 1]).then_inc(s_xin, 1)

            def silu_u(b, o):
                wait(act, s_cv, n(b, o, HALO * E, HALO * E))
                uu = u[o % 2][:].rearrange("p e t -> p (e t)")
                nc.scalar.activation(uu, uu, ACT.Silu).then_inc(s_u, 1)
                nc.scalar.preload_act_table_set(EXP_LN)

            def low(b, o):
                wait(act, s_xp, n(b, o, 1, 1))
                wait(act, s_dtm, n(b, o, E, 0))
                wait(act, s_bcw, n(b, o, 16, 0))
                nc.scalar.copy(xpr[:], pA[0][0:2 * R, :]).then_inc(s_low, 1)

            def softplus(b, o, e):
                k = n(b, o, 2 * E, 2 * e)
                wait(act, s_dtm, n(b, o, E, e + 1))
                wait(act, s_pc, n(b, o, 2 * E, 2 * e))
                bias = dtb[:, e:e + 1]
                nc.scalar.activation(sp3[:, 0, :], pD[:], ACT.Abs, bias=bias).then_inc(s_spa, 1)
                act.wait_ge(s_spa, k + 1)
                nc.scalar.activation(sp3[:, 0, :], sp3[:, 0, :], ACT.Exp, scale=-1.0).then_inc(s_spa, 1)
                act.wait_ge(s_spa, k + 2)
                nc.scalar.activation(sp3[:, 1, :], sp3[:, 0, :], ACT.Identity, bias=1.0)
                nc.scalar.activation(sp3[:, 2, :], sp3[:, 0, :], ACT.Ln, bias=1.0)
                nc.scalar.activation(dt[e % 2][:], pD[:], ACT.Relu, bias=bias).then_inc(s_sp, 1)

            def decays(b, o, g):
                e, q = divmod(g, GQ)
                if q == 0:
                    wait(act, s_pc, n(b, o, 2 * E, 2 * (e + 1)))
                wait(act, s_scan, n(b, o, G, g - (NST - 1)))
                for i in range(GN):
                    s = e * NS + q * GN + i
                    a = nc.scalar.activation(decay[g % NST][:, i, :], dt[e % 2][:], ACT.Exp, scale=an[:, s:s + 1])
                a.then_inc(s_dec, 1)

            def diagonal(b, o, e):
                wait(act, s_skip, n(b, o, E, e - 1))
                nc.scalar.activation(ddiag[e % 2][:], ident, ACT.Copy, scale=dv[:, e:e + 1]).then_inc(s_diag, 1)

            def residual(b, o, e):
                wait(act, s_yT, n(b, o, E, e + 1))
                nc.scalar.copy(xt[:, :, eT(e)], pT[:].rearrange("p (t d) -> p t d", t=TT)).then_inc(s_x2, 1)

            def norm_x2(b, o, t, last=False):
                wait(act, s_rs2, n(b, o, TT, t + 1))
                if last:
                    act.wait_ge(s_xfp, n(b, o, 2 * TT, 2 * (t - 1)))
                nc.scalar.activation(xr[t % 2][:], xt[:, t, :] if last else xr[t % 2][:], ACT.Identity, bias=nb2[:, t:t + 1],
                                     scale=rs2[:, t:t + 1]).then_inc(s_xf, 1)

            def xfT_out(b, o, f, last=False):
                wait(act, s_xfp, n(b, o, 2 * TT, f + 1))
                if last:
                    if f == 0:
                        act.wait_ge(s_skip, n(b, o, E, E))
                    nc.scalar.copy(u[1][:, f, :], (pT if f % 2 else pF)[:]).then_inc(s_xfT, 1)
                else:
                    wait(act, s_lgm, n(b, o, 2 * TT, f))
                    wait(act, s_xfw, n(b, o, 16 * 2 * TT, 16 * f))
                    nc.scalar.copy(xfT[:].rearrange("p k t -> p (k t)"), pF[:]).then_inc(s_xfT, 1)

            def gate_silu(b, o, part):
                if part == 0:
                    wait(act, s_cur, n(b, o, 1, 1))
                wait(act, s_zx, n(b, o, 32, 16 * (part + 1)))
                for i in range(E // 2):
                    e = part * (E // 2) + i
                    nc.scalar.activation(sz[:, i, :], sz[:, i, :], ACT.Silu, bias=cur[:, 1, e:e + 1],
                                         scale=cur[:, 0, e:e + 1]).then_inc(s_sz, 1)
                nc.scalar.preload_act_table_set(EXP_LN)

            def router_exp(b, o):
                wait(act, s_sm, n(b, o, 6, 3))
                nc.scalar.activation(lg[:], lg[:], ACT.Exp).then_inc(s_ex, 1)

            def late(b, o, g, began, least=0):
                for e, k in at(RES_SLOT, g, began):
                    if k >= least:
                        residual(b, o - k, e)
                for f, k in at(XFT_SLOT, g, began):
                    if k >= least:
                        xfT_out(b, o - k, f, k == least)
                for t, k in at(XF_SLOT, g, began):
                    if k >= least:
                        norm_x2(b, o - k, t, k == least)
                for _, k in at(EXP_SLOT, g, began):
                    if k >= least:
                        router_exp(b, o - k)

            def half(b, o, began):
                for g in range(G):
                    decays(b, o, g)
                    for e, k in at(DIAG_SLOT, g, began):
                        diagonal(b, o - k, e)
                    for j, k in at(XIN_SLOT, g, began):
                        xin_ready(b, o - k, j)
                    for _, k in at(SILU_SLOT, g, began):
                        silu_u(b, o - k)
                    for _, k in at(LOW_SLOT, g, began):
                        low(b, o - k)
                    for e, k in at(SP_SLOT, g, began):
                        softplus(b, o - k, e)
                    for part, k in at(SZ_SLOT, g, began):
                        gate_silu(b, o - k, part)
                    late(b, o, g, began)

            act.wait_ge(s_w, 16 * NW)
            nc.scalar.activation(al[:], al[:], ACT.Exp).then_inc(s_c, 1)
            nc.scalar.activation(tg[:], gg[:], ACT.Tanh).then_inc(s_c, 1)
            nc.scalar.preload_act_table_set(EXP_LN)
            act.wait_ge(s_c, 6)
            for j in range(E):
                xin_ready(0, 0, j)
            silu_u(0, 0)
            low(0, 0)
            softplus(0, 0, 0)
            softplus(0, 0, 1)
            for h in range(HB):
                half(0, h, h)
            with act.Fori(1, B) as b:
                for h in range(HB):
                    half(b, h, 2)

            W_BESIDE = [(), (0, 1, 2), (3, 4, 5), (6, 7)]

            def high_w(k):
                act.wait_ge(s_cut, k + 1)
                nc.scalar.copy(whi[:, k, :], cut[k % 2]).then_inc(s_hi, 1)

            def high_tile(t, k):
                act.wait_ge(s_cut, k + (E + 1))
                wait(act, s_mm, k - 1)
                nc.scalar.copy(thi[t % 2][:], cut[t % 2]).then_inc(s_hi, 1)

            for h in range(HB):
                for g in range(G):
                    late(B, h, g, 2, h + 1)
                    for t, k in at(XF_SLOT, g, 2):
                        if k == h + 1:
                            for m in W_BESIDE[t]:
                                high_w(m)
            def product_out(t, k, cc):
                act.wait_ge(s_mm, k + 1)
                if not isinstance(cc, int) or cc:
                    act.wait_ge(s_out[t], 16 * cc)
                for hh in range(2):
                    z = nc.scalar.copy(ot[t][:, hh * 512:(hh + 1) * 512], pC[t % 2][hh][:])
                z.then_inc(s_ev, 1)

            high_tile(0, 0)
            high_tile(1, 1)
            for t in range(TT):
                product_out(t, t, 0)
                high_tile((t + 2) % TT, t + 2)
            with act.Fori(1, NC - 1) as c:
                for t in range(TT):
                    product_out(t, c * TT + t, c)
                    high_tile((t + 2) % TT, c * TT + (t + 2))
            for t in range(TT):
                product_out(t, (NC - 1) * TT + t, NC - 1)
                if t < 2:
                    high_tile(t + 2, (NC - 1) * TT + (t + 2))

        @block.vector
        def _(dve):
            def conv(b, o, j, i):
                if i == 0:
                    wait(dve, s_xin, n(b, o, E, j + 1))
                else:
                    dve.wait_ge(s_cv, n(b, o, HALO * E, HALO * j + i))
                nc.vector.scalar_tensor_tensor(out=u[o % 2][:, j, :], in0=xin[j % 2][:, i:i + T],
                                               scalar=cw[:, j, i:i + 1], in1=u[o % 2][:, j, :],
                                               op0=ALU.mult, op1=ALU.add).then_inc(s_cv, 1)

            def log1p_rest(b, o, e):
                wait(dve, s_sp, n(b, o, E, e + 1))
                nc.vector.scalar_tensor_tensor(out=sp3[:, 1, :], in0=sp3[:, 1, :], scalar=-1.0, in1=sp3[:, 0, :],
                                               op0=ALU.add, op1=ALU.subtract).then_inc(s_e1, 1)

            def input_of(b, o, g, i):
                e, q = divmod(g, GQ)
                if i == 0:
                    if q == 0:
                        wait(dve, s_dt, n(b, o, E, e + 1))
                    if e == 0:
                        wait(dve, s_bcq[q], n(b, o, 32, 32))
                wait(dve, s_ns, n(b, o, GN * G, GN * (g - NST) + i + 1))
                nc.vector.tensor_tensor(state_of(o, g)[:, i, :], dtu[e % 2][:], bbc[:, GN * q + i, :], ALU.mult) \
                    .then_inc(s_dbu, 1)

            def keep_carry(b, o, g):
                e, q = divmod(g, GQ)
                dve.wait_ge(s_scan, n(b, o, G, g + 1))
                nc.vector.tensor_copy(carry[:, e, q * GN:(q + 1) * GN], state_of(o, g)[:, :, T - 1]).then_inc(s_carry, 1)

            def group(b, o, g):
                e, q = divmod(g, GQ)
                input_of(b, o, g, 0)
                if g and o % HB == 0:
                    keep_carry(b, o, g - 1)
                elif g == 0 and o % HB == 1:
                    keep_carry(b, o - 1, G - 1)
                for i in range(1, GN):
                    input_of(b, o, g, i)
                st = state_of(o, g)
                for i in range(GN):
                    dve.wait_ge(s_dbu, n(b, o, GN * G, GN * g + i + 1))
                    if i == 0:
                        wait(dve, s_dec, n(b, o, G, g + 1))
                    s = q * GN + i
                    sc = nc.vector.tensor_tensor_scan(st[:, i, :], decay[g % NST][:, i, :], st[:, i, :],
                                                      0.0 if o % HB == 0 else carry[:, e, s:s + 1],
                                                      ALU.mult, ALU.add)
                sc.then_inc(s_scan, 1)

            def y_out(b, o, e):
                wait(dve, s_skip, n(b, o, E, e + 1))
                wait(dve, s_sz, n(b, o, E, e + 1))
                wait(dve, s_yT, n(b, o, E, e))
                nc.vector.tensor_tensor(y[:], pY[e % 2][:], sz[:, e % (E // 2), :], ALU.mult).then_inc(s_y, 1)

            def ln1_stats(j):
                if j >= 2:
                    dve.wait_ge(s_ln1, 2 * (j - 1))
                dve.wait_ge(s_stage[j], 16 * TT)
                for t in range(TT):
                    for i in range(2):
                        z = nc.vector.bn_stats(stats[j % 2][:, t, i, :], stage[j * TT + t][:, i * 512:(i + 1) * 512])
                z.then_inc(s_ln1, 1)
                dve.wait_ge(s_ln1, 2 * j + 1)
                for t in range(TT):
                    k = j * TT + t
                    z = nc.vector.bn_aggr(mv1[:, k // E, k % E, :], stats[j % 2][:, t, :, :].rearrange("p a s -> p (a s)"))
                z.then_inc(s_ln1, 1)

            def ln1_bias():
                dve.wait_ge(s_rs1, 1)
                nc.vector.scalar_tensor_tensor(out=ln1[:, :, 1, :], in0=mv1[:, :, :, 0], scalar=-1.0, in1=ln1[:, :, 0, :],
                                               op0=ALU.mult, op1=ALU.mult).then_inc(s_ln1b, 1)
                dve.wait_ge(s_ln1b, 2)

            def row_ln1(b, o):
                wait(dve, s_sz, n(b, o, E, 0))
                nc.vector.tensor_scalar(cur[:], ln1[:, b, :, :], 1.0, None, ALU.mult).then_inc(s_cur, 1)

            def ln2_stats(b, o, t, last=False):
                k = n(b, o, 3 * TT, 3 * t)
                if last:
                    dve.wait_ge(s_x2, n(b, o, E, E))
                else:
                    wait(dve, s_xr[t % 2], n(b, o, 16 * TT // 2, 16 * (t // 2 + 1)))
                src = xt[:, t, :] if last else xr[t % 2][:]
                for i in range(2):
                    z = nc.vector.bn_stats(stats[0][:, t, i, :], src[:, i * 512:(i + 1) * 512])
                z.then_inc(s_bn, 1)
                dve.wait_ge(s_bn, k + 1)
                nc.vector.memset(small[:, 15:16], 0.0)
                nc.vector.bn_aggr(mv2[:, t, :], stats[0][:, t, :, :].rearrange("p a s -> p (a s)")).then_inc(s_bn, 1)
                dve.wait_ge(s_bn, k + 2)
                nc.vector.tensor_scalar(nm2[:, t:t + 1], mv2[:, t, 0:1], -1.0, None, ALU.mult)
                nc.vector.tensor_scalar(ve2[:, t:t + 1], mv2[:, t, 1:2], EPS, None, ALU.add).then_inc(s_bn, 1)

            def softmax_in(b, o):
                wait(dve, s_lgm, n(b, o, 2 * TT, 2 * TT))
                nc.vector.tensor_tensor(lg[:], pL[:, 0:TT * NX].rearrange("p (t s) -> p t s", t=TT), rb[:], ALU.add) \
                    .then_inc(s_sm, 1)
                dve.wait_ge(s_sm, n(b, o, 6, 1))
                nc.vector.tensor_reduce(mx[:], lg[:], AX.X, ALU.max).then_inc(s_sm, 1)
                dve.wait_ge(s_sm, n(b, o, 6, 2))
                nc.vector.tensor_tensor(lg[:], lg[:], mx[:].rearrange("p (t a) -> p t a", a=1).broadcast_to([P, TT, NX]),
                                        ALU.subtract).then_inc(s_sm, 1)

            def softmax_out(b, o):
                wait(dve, s_ex, n(b, o, 1, 1))
                nc.vector.tensor_reduce(sm[:], lg[:], AX.X, ALU.add).then_inc(s_sm, 1)
                dve.wait_ge(s_sm, n(b, o, 6, 4))
                nc.vector.reciprocal(rc[:], sm[:]).then_inc(s_sm, 1)
                dve.wait_ge(s_sm, n(b, o, 6, 5))
                nc.vector.tensor_tensor(S_tok[:, :, b * HB + o, :], lg[:],
                                        rc[:].rearrange("p (t a) -> p t a", a=1).broadcast_to([P, TT, NX]),
                                        ALU.mult).then_inc(s_sm, 1)

            def late(b, o, g, began, least=0):
                for e, k in at(Y_SLOT, g, began):
                    if k >= least:
                        y_out(b, o - k, e)
                for t, k in at(LN2_SLOT, g, began):
                    if k >= least:
                        ln2_stats(b, o - k, t, k == least)
                for _, k in at(SMI_SLOT, g, began):
                    if k >= least:
                        softmax_in(b, o - k)
                for _, k in at(SMO_SLOT, g, began):
                    if k >= least:
                        softmax_out(b, o - k)

            def half(b, o, began):
                for g in range(G):
                    group(b, o, g)
                    for i in range(HALO):
                        for j, k in at([s + i for s in CONV_SLOT], g, began):
                            conv(b, o - k, j, i)
                    for e, k in at(REST_SLOT, g, began):
                        log1p_rest(b, o - k, e)
                    late(b, o, g, began)
                    if g == 4:
                        if not began:
                            ln1_bias()
                        row_ln1(b, o)

            nc.vector.memset(zero3[:], 0.0).then_inc(s_c, 1)
            nc.vector.memset(mhalf[:], -0.5).then_inc(s_c, 1)
            dve.wait_ge(s_w, 16 * NW)
            dve.wait_ge(s_c, 4)
            nc.vector.tensor_scalar(an[:], al[:], -1.0, None, ALU.mult).then_inc(s_c, 1)
            nc.vector.tensor_scalar(tgid[:], ident, tg[:, 0:1], None, ALU.mult).then_inc(s_c, 1)
            for j in range(E):
                for i in range(HALO):
                    conv(0, 0, j, i)
                if j % 2:
                    ln1_stats(j // 2)
            for j in range(E // 2, E - 1):
                ln1_stats(j)
            log1p_rest(0, 0, 0)
            ln1_stats(E - 1)
            dve.wait_ge(s_ln1, 2 * E)
            nc.vector.tensor_scalar(ve1[:], mv1[:, :, :, 1], EPS, None, ALU.add).then_inc(s_ln1b, 1)
            log1p_rest(0, 0, 1)
            for h in range(HB):
                half(0, h, h)
            with dve.Fori(1, B) as b:
                for h in range(HB):
                    half(b, h, 2)

            def high_bits(dst, src):
                return nc.vector.tensor_scalar(dst.bitcast(U32), src.bitcast(U32), LOW_BITS, LOW_BITS,
                                               ALU.logical_shift_right, ALU.logical_shift_left)

            def cut_w(k):
                dve.wait_ge(s_wr[k % 4], 16 * (k // 4 + 1))
                if k == 0:
                    dve.wait_ge(s_ctx, n(B, 1, 16, 16))
                wait(dve, s_hi, k - 1)
                wait(dve, s_lo, k - 1)
                high_bits(cut[k % 2], wraw[k % 4]).then_inc(s_cut, 1)

            def cut_tile(t, k, cc):
                dve.wait_ge(s_lx[t], (cc + 1) * 16)
                dve.wait_ge(s_hi, k + (E - 1))
                dve.wait_ge(s_lo, k + (E - 1))
                high_bits(cut[t % 2], lt[t]).then_inc(s_cut, 1)

            for h in range(HB):
                for g in range(G):
                    late(B, h, g, 2, h + 1)
                    for t, k in at(LN2_SLOT, g, 2):
                        if k == h + 1 and t == TT - 1:
                            for m in range(E):
                                cut_w(m)

            thr, bit, cand, step = (bits[:, i:i + 1] for i in range(4))
            dve.wait_ge(s_srt, 1)
            dve.wait_ge(s_ns, n(B, 0, GN * G, 0))
            for t in range(TT):
                cut_tile(t, t, 0)
            nc.vector.tensor_copy(srt, pF[:]).then_inc(s_b, 1)
            nc.vector.memset(thr, 0)
            nc.vector.memset(ones, 1.0)
            nc.vector.memset(bit, 1 << (BITS - 1)).then_inc(s_b, 1)
            def search(i):
                dve.wait_ge(s_b, i * 4 + 2)
                nc.vector.tensor_tensor(cand, thr, bit, ALU.bitwise_or).then_inc(s_b, 1)
                dve.wait_ge(s_b, i * 4 + 3)
                nc.vector.tensor_scalar(junk, srt, cand.bitcast(F32), 0.0, ALU.is_ge, ALU.add,
                                        accum_out=small[:, 0:1]).then_inc(s_b, 1)
                dve.wait_ge(s_cnt, i + 1)
                nc.vector.scalar_tensor_tensor(out=step, in0=pD[:, 0:1], scalar=float(TOPK), in1=bit,
                                               op0=ALU.is_ge, op1=ALU.mult).then_inc(s_b, 1)
                dve.wait_ge(s_b, i * 4 + 5)
                nc.vector.tensor_scalar(bit, bit, 1, None, ALU.logical_shift_right)
                nc.vector.tensor_tensor(thr, thr, step, ALU.bitwise_or).then_inc(s_b, 1)

            parts = [0, 10, 18, 26, BITS]
            for p in range(4):
                with dve.Fori(parts[p], parts[p + 1]) as i:
                    search(i)
                if p < 3:
                    cut_tile(p, TT + p, 1)
            dve.wait_ge(s_b, BITS * 4 + 2)
            thf = thr.bitcast(F32)
            nc.vector.tensor_scalar(gtm, srt, thf, 0.0, ALU.is_gt, ALU.add, accum_out=small[:, 1:2])
            nc.vector.tensor_scalar(eqm, srt, thf, None, ALU.is_equal).then_inc(s_sel, 1)
            dve.wait_ge(s_sel, 1)
            nc.vector.tensor_tensor_scan(cum, ones, eqm, 0.0, ALU.mult, ALU.add).then_inc(s_sel, 2)
            dve.wait_ge(s_sp2, 1)
            nc.vector.tensor_scalar(small[:, 3:4], pD[:, 2:3], -1.0, float(TOPK), ALU.mult, ALU.add).then_inc(s_sel, 1)
            dve.wait_ge(s_sel, 4)
            nc.vector.tensor_tensor(small[:, 4:5], small[:, 3:4], pD[:, 4:5], ALU.subtract).then_inc(s_sel, 1)
            dve.wait_ge(s_sel, 5)
            nc.vector.scalar_tensor_tensor(out=sele, in0=cum, scalar=small[:, 4:5], in1=eqm,
                                           op0=ALU.is_le, op1=ALU.mult).then_inc(s_sel, 1)
            dve.wait_ge(s_sel, 6)
            nc.vector.tensor_tensor(sele, sele, gtm, ALU.add).then_inc(s_sel, 1)
            dve.wait_ge(s_sel, 7)
            nc.vector.tensor_tensor(sele, sele, srt, ALU.mult).then_inc(s_sel, 1)
            dve.wait_ge(s_sp2, 2)
            nc.vector.tensor_scalar(coef[:], pL[:, 0:TT * NC].rearrange("p (t c) -> p t c", t=TT), tg[:, 1:2], None,
                                    ALU.mult).then_inc(s_sel, 1)
            dve.wait_ge(s_sel, 9)
            dve.wait_ge(s_big, 16)

            def finish(t, k, cc):
                dve.wait_ge(s_ev, k + 1)
                nc.vector.tensor_tensor(ot[t], ot[t], ebias, ALU.add).then_inc(s_o1, 1)
                dve.wait_ge(s_o1, k + 1)
                dve.wait_ge(s_l2[t], (cc + 1) * 16)
                nc.vector.scalar_tensor_tensor(out=ot[t], in0=ot[t], scalar=coef[:, t, cc:cc + 1] if isinstance(cc, int)
                                               else coef[:, t, bass.ds(cc, 1)], in1=x2t[t],
                                               op0=ALU.mult, op1=ALU.add).then_inc(s_o, 1)

            for t in range(TT):
                finish(t, t, 0)
            cut_tile(TT - 1, 2 * TT - 1, 1)
            with dve.Fori(1, NC - 1) as c:
                for t in range(TT):
                    finish(t, c * TT + t, c)
                    cut_tile(t, (c + 1) * TT + t, c + 1)
            for t in range(TT):
                finish(t, (NC - 1) * TT + t, NC - 1)

        @block.gpsimd
        def _(pool):
            def dt_block(b, o, e, step):
                k = n(b, o, 2 * E, 2 * e)
                if step == 0:
                    wait(pool, s_e1, n(b, o, E, e + 1))
                    nc.gpsimd.tensor_tensor(sp3[:, 2, :], sp3[:, 2, :], sp3[:, 1, :], ALU.subtract).then_inc(s_pc, 1)
                elif step == 1:
                    pool.wait_ge(s_pc, k + 1)
                    nc.gpsimd.tensor_tensor(dt[e % 2][:], dt[e % 2][:], sp3[:, 2, :], ALU.add).then_inc(s_pc, 1)
                else:
                    pool.wait_ge(s_pc, k + 2)
                    wait(pool, s_dbu, n(b, o, GN * G, GN * GQ * (e - 1)))
                    nc.gpsimd.tensor_tensor(dtu[e % 2][:], dt[e % 2][:], u[o % 2][:, e, :], ALU.mult).then_inc(s_dt, 1)

            def times_c(b, o, g):
                e, q = divmod(g, GQ)
                if e == 0:
                    wait(pool, s_bcq[q], n(b, o, 32, 32))
                if o % HB == 0:
                    wait(pool, s_carry, b * G + (g + 1))
                else:
                    wait(pool, s_scan, n(b, o, G, g + 1))
                st = state_of(o, g)
                nc.gpsimd.tensor_tensor(st[:], st[:], cbc[:, GN * q:GN * (q + 1), :], ALU.mult).then_inc(s_hc, 1)

            def rstd2(b, o, t):
                wait(pool, s_bn, n(b, o, 3 * TT, 3 * t + 3))
                nc.gpsimd.tensor_tensor(rs2[:, t:t + 1], ve2[:, t:t + 1], mhalf[:, 0, 0:1], ALU.pow).then_inc(s_pr, 1)
                pool.wait_ge(s_pr, n(b, o, TT, t + 1))
                nc.gpsimd.tensor_tensor(nb2[:, t:t + 1], nm2[:, t:t + 1], rs2[:, t:t + 1], ALU.mult).then_inc(s_rs2, 1)

            def late(b, o, g, began, least=0):
                for t, k in at(RS_SLOT, g, began):
                    if k >= least:
                        rstd2(b, o - k, t)

            def half(b, o, began):
                for g in range(G):
                    times_c(b, o, g)
                    for step in range(3):
                        for e, k in at([s + step for s in DT_SLOT], g, began):
                            dt_block(b, o - k, e, step)
                    late(b, o, g, began)

            pool.wait_ge(s_c, 5)
            for step in range(3):
                dt_block(0, 0, 0, step)
            pool.wait_ge(s_ln1b, 1)
            nc.gpsimd.tensor_tensor(ln1[:, :, 0, :], ve1[:], mhalf[:], ALU.pow).then_inc(s_rs1, 1)
            dt_block(0, 0, 1, 0)
            for h in range(HB):
                half(0, h, h)
            with pool.Fori(1, B) as b:
                for h in range(HB):
                    half(b, h, 2)

            def low_w(k):
                pool.wait_ge(s_cut, k + 1)
                nc.gpsimd.tensor_tensor(wlo[:, k, :], wraw[k % 4], cut[k % 2], ALU.subtract).then_inc(s_lo, 1)

            def low_tile(t, k):
                pool.wait_ge(s_cut, k + (E + 1))
                wait(pool, s_mm, k - 1)
                nc.gpsimd.tensor_tensor(tlo[t % 2][:], lt[t], cut[t % 2], ALU.subtract).then_inc(s_lo, 1)

            for h in range(HB):
                for g in range(G):
                    late(B, h, g, 2, h + 1)
                    for t, k in at(RS_SLOT, g, 2):
                        if k == h + 1 and t == TT - 1:
                            for m in range(E):
                                low_w(m)
            for t in range(TT):
                low_tile(t, t)
            with pool.Fori(1, NC) as c:
                for t in range(TT):
                    low_tile(t, c * TT + t)


def _row_masks():
    seg, ex = np.arange(P) // NX, np.arange(P) % NX
    same = ex[:, None] == ex[None, :]
    early = same & (seg[:, None] < seg[None, :])
    of = seg[:, None] == np.arange(NC)[None, :]
    return np.concatenate([same, early, of], axis=1).astype(np.float32)


def by_block(w):
    return np.moveaxis(w.reshape(E, P, *w.shape[1:]), 0, 1)


def kernel(**inputs):
    import concourse.bacc as _bacc
    from concourse.bass_utils import run_bass_kernel_spmd as _run

    a = {k: np.asarray(v) for k, v in inputs.items()}
    ctx = a["ctx_1024"].reshape(NC, T, KC, P).transpose(0, 3, 2, 1)
    arrays = {
        "x": a["x"].reshape(NC, T, D),
        "ctxT": np.concatenate([ctx, ctx[:2]], axis=0),
        "g_xattn": a["g_xattn"],
        "g_ffn": a["g_ffn"],
        "winT": a["L0_xattn_in_proj_w"].reshape(E, P, KC, P).transpose(0, 3, 2, 1),
        "conv_w": by_block(a["L0_xattn_conv_w"].reshape(D, TAPS)),
        "conv_b": by_block(a["L0_xattn_conv_b"]),
        "xpT": by_block(a["L0_xattn_x_proj_w"].T),
        "dtpT": a["L0_xattn_dt_proj_w"].reshape(E, P, R).transpose(0, 2, 1),
        "dt_b": by_block(a["L0_xattn_dt_proj_b"]),
        "a_log": by_block(a["L0_xattn_A_log"]).reshape(P, E * NS),
        "dvec": by_block(a["L0_xattn_D"]),
        "router_w": by_block(a["L0_ffn_router_w"]),
        "router_b": a["L0_ffn_router_b"],
        "expert_w": a["L0_ffn_expert_w"],
        "expert_b": a["L0_ffn_expert_b"],
        "consts": np.eye(P, dtype=np.float32),
        "row_masks": _row_masks(),
    }
    arrays = {k: np.ascontiguousarray(v) for k, v in arrays.items()}
    nc = _bacc.Bacc("TRN2", target_bir_lowering=False, num_devices=1)
    args = [nc.dram_tensor(f"in_{k}", v.shape, mybir.dt.from_np(v.dtype), kind="ExternalInput").ap()
            for k, v in arrays.items()]
    o = nc.dram_tensor("out", (NC, T, D), F32, kind="ExternalOutput").ap()
    mamba_moe(nc, *args, o)
    r = _run(nc, [{f"in_{k}": v for k, v in arrays.items()}], core_ids=[0])
    return r.results[0]["out"].reshape(B, L, D)
```
